# Optimizing a Trainium2 kernel written in Bass

```python
import numpy as np
import jax
import jax.numpy as jnp

def _softmax(x, axis=-1):
    return jax.nn.softmax(x, axis=axis)

def _gelu(x):
    return jax.nn.gelu(x, approximate=True)

def _silu(x):
    return jax.nn.silu(x)

def _sigmoid(x):
    return jax.nn.sigmoid(x)

def _layernorm(x, axis=-1, eps=1e-05):
    m = jnp.mean(x, axis=axis, keepdims=True)
    v = jnp.var(x, axis=axis, keepdims=True)
    return (x - m) / jnp.sqrt(v + eps)

def _scatter_add(tgt, idx, src, axis=0):
    return tgt.at[idx].add(src)

def _segment_sum(src, seg, n):
    return jax.ops.segment_sum(src, seg, n)
kernel_name = 'mk_gnn_resnorm_d2_gnn_r8_538fb1'

def setup_inputs(seed: int=0):
    np.random.seed(seed)
    _w = jnp.asarray

    def _rec_inputs():
        import jax
        import jax.numpy as jnp
        _gk = jax.random.key(seed)
        x = -0.0005121 + 1.001 * jax.random.normal(jax.random.fold_in(_gk, 1), (6250, 64), jnp.float32)
        _s = jax.random.randint(jax.random.fold_in(_gk, 2), (100000,), 0, 6250, jnp.int32)
        _d = jax.random.randint(jax.random.fold_in(_gk, 3), (100000,), 0, 6250, jnp.int32)
        _loop = jnp.arange(6250, dtype=jnp.int32)
        src = jnp.concatenate([_s, _d, _loop])
        dst = jnp.concatenate([_d, _s, _loop])
        _o = jnp.argsort(dst, stable=True)
        src = src[_o]
        dst = dst[_o]
        edge_attr_64 = -5.3897e-05 + 0.999841 * jax.random.normal(jax.random.fold_in(_gk, 11), (206250, 64), jnp.float32)
        return (x, src, dst, edge_attr_64)
    x, src, dst, edge_attr_64 = _rec_inputs()

    def _L0_gnn_setup():
        import jax, jax.numpy as jnp
        import numpy as np
        N_NODES = 6250
        N_EDGES = 50000
        DIM = 64
        HEADS = 4
        BN_EPS = 1e-05

        def glorot(key, shape, fan_in, fan_out):
            std = np.sqrt(6.0 / (fan_in + fan_out))
            return jax.random.uniform(key, shape, jnp.float32, -std, std)

        def segment_softmax(a, seg, num_segments):
            m = jax.ops.segment_max(a, seg, num_segments=num_segments)
            e = jnp.exp(a - m[seg])
            s = jax.ops.segment_sum(e, seg, num_segments=num_segments)
            return e / (s[seg] + 1e-16)
        key = jax.random.key(seed)
        ks = jax.random.split(key, 6)
        x = jax.random.normal(ks[0], (N_NODES, DIM), jnp.float32)
        edge_attr = jax.random.normal(ks[1], (N_EDGES, DIM), jnp.float32)
        edge_index = jax.random.randint(ks[2], (2, N_EDGES), 0, N_NODES, jnp.int64)
        W = glorot(ks[3], (2 * DIM, HEADS * DIM), 2 * DIM, HEADS * DIM)
        att = glorot(ks[4], (1, HEADS, 2 * DIM), 2 * DIM, 1)
        bias = jnp.zeros((DIM,), jnp.float32)
        bn_gamma = jnp.ones((HEADS,), jnp.float32)
        bn_beta = jnp.zeros((HEADS,), jnp.float32)
        return {'x': x, 'edge_attr': edge_attr, 'W': W, 'att': att, 'bias': bias, 'bn_gamma': bn_gamma, 'bn_beta': bn_beta, 'edge_index': edge_index}
    _L0_gnn_all = _L0_gnn_setup()
    _L0_gnn_in = {k: v for k, v in _L0_gnn_all.items() if k in ('W', 'att', 'bias', 'bn_gamma', 'bn_beta')}
    del _L0_gnn_all

    def _L1_gnn_setup():
        import jax, jax.numpy as jnp
        import numpy as np
        N_NODES = 12500

        def gcn_conv(x, src, dst, W, b):
            n = x.shape[0]
            h = x @ W
            ones = jnp.ones(src.shape[0], dtype=x.dtype)
            deg = jax.ops.segment_sum(ones, dst, num_segments=n)
            dinv = jnp.where(deg > 0, jax.lax.rsqrt(deg), 0.0)
            norm = dinv[src] * dinv[dst]
            msgs = h[src] * norm[:, None]
            out = jax.ops.segment_sum(msgs, dst, num_segments=n)
            return out + b
        key = jax.random.key(seed)
        ks = jax.random.split(key, 4)
        d = 64
        n_edges = 156250
        x = jax.random.normal(ks[0], (N_NODES, d), dtype=jnp.float32)
        edge_index = jax.random.randint(ks[1], (2, n_edges), 0, N_NODES, dtype=jnp.int64)
        W1 = jax.random.normal(ks[2], (d, d), dtype=jnp.float32) / np.sqrt(d)
        b1 = jnp.zeros((d,), dtype=jnp.float32)
        W2 = jax.random.normal(ks[3], (d, d), dtype=jnp.float32) / np.sqrt(d)
        b2 = jnp.zeros((d,), dtype=jnp.float32)
        return {'x': x, 'edge_index': edge_index, 'W1': W1, 'b1': b1, 'W2': W2, 'b2': b2}
    _L1_gnn_all = _L1_gnn_setup()
    _L1_gnn_in = {k: v for k, v in _L1_gnn_all.items() if k in ('W1', 'b1', 'W2', 'b2')}
    del _L1_gnn_all
    return {'x': x, 'src': src, 'dst': dst, 'edge_attr_64': edge_attr_64, 'L0_gnn_W': _L0_gnn_in['W'], 'L0_gnn_att': _L0_gnn_in['att'], 'L0_gnn_bias': _L0_gnn_in['bias'], 'L0_gnn_bn_gamma': _L0_gnn_in['bn_gamma'], 'L0_gnn_bn_beta': _L0_gnn_in['bn_beta'], 'L1_gnn_W1': _L1_gnn_in['W1'], 'L1_gnn_b1': _L1_gnn_in['b1'], 'L1_gnn_W2': _L1_gnn_in['W2'], 'L1_gnn_b2': _L1_gnn_in['b2']}

def reference(x, src, dst, edge_attr_64, L0_gnn_W, L0_gnn_att, L0_gnn_bias, L0_gnn_bn_gamma, L0_gnn_bn_beta, L1_gnn_W1, L1_gnn_b1, L1_gnn_W2, L1_gnn_b2):
    import jax
    import jax.numpy as jnp

    def _L0_gnn_ref(x, edge_attr, W, att, bias, bn_gamma, bn_beta, edge_index):
        import jax, jax.numpy as jnp
        import numpy as np
        N_NODES = 6250
        N_EDGES = 50000
        DIM = 64
        HEADS = 4
        BN_EPS = 1e-05

        def glorot(key, shape, fan_in, fan_out):
            std = np.sqrt(6.0 / (fan_in + fan_out))
            return jax.random.uniform(key, shape, jnp.float32, -std, std)

        def segment_softmax(a, seg, num_segments):
            m = jax.ops.segment_max(a, seg, num_segments=num_segments)
            e = jnp.exp(a - m[seg])
            s = jax.ops.segment_sum(e, seg, num_segments=num_segments)
            return e / (s[seg] + 1e-16)
        act = jax.nn.softplus
        i, j = (edge_index[0], edge_index[1])
        x_i = x[i]
        x_j = x[j]
        out_i = act(jnp.concatenate([x_i, edge_attr], -1) @ W).reshape(-1, HEADS, DIM)
        out_j = act(jnp.concatenate([x_j, edge_attr], -1) @ W).reshape(-1, HEADS, DIM)
        alpha = act((jnp.concatenate([out_i, out_j], -1) * att).sum(-1))
        mu = alpha.mean(0)
        var = alpha.var(0)
        alpha = (alpha - mu) * jax.lax.rsqrt(var + BN_EPS) * bn_gamma + bn_beta
        alpha = act(alpha)
        alpha = segment_softmax(alpha, i, N_NODES)
        msg = out_j * alpha[:, :, None]
        aggr = jax.ops.segment_sum(msg, i, num_segments=N_NODES)
        out = aggr.mean(1) + bias
        return out

    def _L1_gnn_ref(x, edge_index, W1, b1, W2, b2):
        import jax, jax.numpy as jnp
        import numpy as np
        N_NODES = 12500

        def gcn_conv(x, src, dst, W, b):
            n = x.shape[0]
            h = x @ W
            ones = jnp.ones(src.shape[0], dtype=x.dtype)
            deg = jax.ops.segment_sum(ones, dst, num_segments=n)
            dinv = jnp.where(deg > 0, jax.lax.rsqrt(deg), 0.0)
            norm = dinv[src] * dinv[dst]
            msgs = h[src] * norm[:, None]
            out = jax.ops.segment_sum(msgs, dst, num_segments=n)
            return out + b
        n = x.shape[0]
        loop = jnp.arange(n, dtype=edge_index.dtype)
        src = jnp.concatenate([edge_index[0], loop])
        dst = jnp.concatenate([edge_index[1], loop])
        h = gcn_conv(x, src, dst, W1, b1)
        h = gcn_conv(h, src, dst, W2, b2)
        return jax.nn.relu(h)
    edge_index = jnp.stack([src, dst])
    x = _layernorm(x + _L0_gnn_ref(x, edge_attr_64, L0_gnn_W, L0_gnn_att, L0_gnn_bias, L0_gnn_bn_gamma, L0_gnn_bn_beta, edge_index), axis=-1)
    x = _layernorm(x + _L1_gnn_ref(x, edge_index, L1_gnn_W1, L1_gnn_b1, L1_gnn_W2, L1_gnn_b2), axis=-1)
    return x

_drawn_inputs = setup_inputs


def setup_inputs(seed=0):
    import zlib

    import numpy as np

    out = dict(_drawn_inputs(seed))
    spreads = {'L0_gnn_bias': (0.0, 0.1),
     'L0_gnn_bn_gamma': (1.0, 0.6),
     'L0_gnn_bn_beta': (0.0, 0.8),
     'L1_gnn_b1': (0.0, 0.1),
     'L1_gnn_b2': (0.0, 0.1)}
    factors = {}
    for name, (base, spread) in spreads.items():
        noise = np.random.default_rng([zlib.crc32(name.encode()), seed]).standard_normal(out[name].shape)
        drawn = base * np.exp(spread * noise) if base else spread * noise
        out[name] = jnp.asarray(drawn.astype(out[name].dtype))
    for name, factor in factors.items():
        out[name] = (out[name] * factor).astype(out[name].dtype)
    return out
```

```python
import concourse.bass as bass
from concourse import mybir
from contextlib import ExitStack

fp32 = mybir.dt.float32
bf16 = mybir.dt.bfloat16
i32 = mybir.dt.int32
ALU = mybir.AluOpType
ACT = mybir.ActivationFunctionType
AX = mybir.AxisListType

P = 128
D = 64
H = 4
C = H * D
K = 8
UT = 2
BU = 4
BC = 7
CAP_SP = 20.0
BN_EPS = 1e-5
LN_EPS = 1e-5


class Sizes:

    def __init__(self, nodes, edges):
        self.N, self.E = nodes, edges
        self.NB = -(-nodes // (P * BC)) * BC
        self.HB = self.NB + 1
        self.NG = 2 * -(-edges // (2 * P * K))
        self.rem = edges - (self.NG - 1) * P * K
        assert self.rem > 0 and self.rem < P * K and self.rem % K
        units = (self.NG * P * K + self.HB * (P * UT - 1)) // (P * UT)
        self.NU = (-(-units // BU) | 1) * BU
        self.TT = self.NU * UT
        self.UC = max(2, -(-self.NU // P))


class Count:

    def __init__(self):
        self.n = 0

    def up(self):
        self.n += 1
        return self.n


def seg(i, j, depth):
    return (i + 1, j - depth) if j >= depth else (i, j)


def gnn_kernel(nc, x, src, dst, ea, W, att, bias, gamma, beta, W1, b1, W2, b2, out):
    z = Sizes(x.shape[0], src.shape[0])
    NB, HB = z.NB, z.HB
    top = ExitStack()
    stages = {}

    def sb(ctx, name, shape, dt):
        return ctx.enter_context(nc.sbuf_tensor(name, shape, dt))

    def ps(ctx, name, shape, dt):
        return ctx.enter_context(nc.psum_tensor(name, shape, dt))

    def sem(ctx, name):
        if ctx not in stages:
            stages[ctx] = []
            ctx.callback(give_back, ctx)
        stages[ctx].append(nc.alloc_semaphore(name))
        return stages[ctx][-1]

    def give_back(ctx):
        nc.clear_and_free_semaphores(stages.pop(ctx))
        nc.all_engine_barrier()

    with top:
        m = {"x_in": x}
        m["rows"] = nc.dram_tensor("rows", (P * z.TT, D + 2), fp32).ap()
        m["rows_d"] = nc.dram_tensor("rows_d", (P * z.TT, 2), fp32).ap()
        m["outj"] = nc.dram_tensor("outj", (P, z.TT * C), fp32).ap()
        m["blk"] = nc.dram_tensor("blk", (2, P * z.UC), i32).ap()
        m["gtab"] = [nc.dram_tensor(f"gtab{n}", (NB * P, D), fp32).ap() for n in range(2)]
        m["io50"] = sb(top, "io50", [P, HB], bf16)
        m["io128"] = sb(top, "io128", [P, P], fp32)
        m["io128b"] = sb(top, "io128b", [P, P], bf16)
        m["pidx"] = sb(top, "pidx", [P, 1], fp32)
        m["ident"] = sb(top, "ident", [P, P], fp32)
        m["identb"] = sb(top, "identb", [P, P], bf16)
        m["tri"] = sb(top, "tri", [P, P], bf16)
        m["onesb"] = sb(top, "onesb", [P, P], bf16)
        m["onesf"] = sb(top, "onesf", [P, P], fp32)
        m["blkS"] = sb(top, "blkS", [1, 2, P * z.UC], i32)
        m["base"] = sb(top, "base", [P, 2, HB], fp32)
        m["deg"] = sb(top, "deg", [P, NB], fp32)
        m["xn"] = sb(top, "xn", [P, NB, D], fp32)
        with ExitStack() as keys:
            key_stage(nc, z, m, keys, sb, ps, sem, x, src, dst)
            sort_stage(nc, z, m, sb, ps, sem, ea)
        with ExitStack() as edge:
            m["loA"] = sb(edge, "loA", [P, z.TT], fp32)
            m["alpha"] = sb(edge, "alpha", [P, z.TT, H], fp32)
            with ExitStack() as ptab:
                m["P3"] = [sb(ptab, f"P3_{n}", [P, HB * C], bf16) for n in range(3)]
                m["Wsb"] = sb(ptab, "Wsb", [P, C], fp32)
                table_stage(nc, z, m, sb, ps, sem, W)
                edge_stage(nc, z, m, sb, ps, sem, att)
            softmax_stage(nc, z, m, sb, ps, sem, gamma, beta)
            m["acc"] = sb(edge, "acc", [P, HB, C + H], fp32)
            message_stage(nc, z, m, sb, ps, sem)
            node_stage(nc, z, m, sb, ps, sem, bias)
        with ExitStack() as conv:
            m["dinv"] = sb(conv, "dinv", [P, NB], fp32)
            m["hn"] = sb(conv, "hn", [P, NB, D], fp32)
            m["gs"] = sb(conv, "gs", [P, NB, D], fp32)
            m["agg"] = sb(conv, "agg", [P, HB, D], fp32)
            for n, (w, b) in enumerate(((W1, b1), (W2, b2))):
                transform_stage(nc, z, m, sb, ps, sem, n, w)
                gather_stage(nc, z, m, sb, ps, sem, n)
                close_stage(nc, z, m, sb, ps, sem, n, b, out)


def key_stage(nc, z, m, keys, sb, ps, sem, x, src, dst):
    NB, HB, NG, T = z.NB, z.HB, z.NG, z.NG * K
    m["hib"] = sb(keys, "hib", [P, 2, T], bf16)
    m["lo"] = sb(keys, "lo", [P, 2, T], fp32)
    m["lob"] = sb(keys, "lob", [P, T], bf16)
    m["val"] = sb(keys, "val", [P, 2, T], i32)
    with ExitStack() as ctx:
        key = sb(ctx, "key", [P, 2, T], i32)
        tmp = sb(ctx, "keytmp", [P, 2, T], i32)
        neg = sb(ctx, "keyneg", [P, 2, T], fp32)
        zer = sb(ctx, "zer", [P, K * HB], bf16)
        oh = [sb(ctx, f"oh{j}", [P, 2, K * HB], bf16) for j in range(2)]
        cnt = sb(ctx, "cnt", [P, 2, HB], fp32)
        cnti = sb(ctx, "cnti", [P, 2, HB], i32)
        uni = sb(ctx, "uni", [P, 2, HB], fp32)
        incl = sb(ctx, "incl", [P, 2, HB], fp32)
        uidx = sb(ctx, "uidx", [P, z.UC], fp32)
        cmp = sb(ctx, "cmp", [P, 2, z.UC, HB], fp32)
        blkf = sb(ctx, "blkf", [P, 2, z.UC], fp32)
        blki = sb(ctx, "blki", [P, 2, z.UC], i32)
        fill = sb(ctx, "fill", [P, 8, D + 2], fp32)
        filld = sb(ctx, "filld", [P, z.TT, 2], fp32)
        psc = [ps(ctx, f"psc{n}", [P, 512], fp32) for n in range(2)]
        made = sem(ctx, "made")
        cleared = sem(ctx, "cleared")
        loaded = sem(ctx, "loaded")
        x_in = sem(ctx, "x_in")
        filled = sem(ctx, "filled")
        v = sem(ctx, "v_key")
        split = sem(ctx, "split")
        oh_ready = [sem(ctx, f"oh_ready{j}") for j in range(2)]
        oh_used = [sem(ctx, f"oh_used{j}") for j in range(2)]
        counted = sem(ctx, "counted")
        blk_ready = sem(ctx, "blk_ready")
        blk_out = sem(ctx, "blk_out")
        block = ctx.enter_context(nc.Block())
        full, tail = z.rem // K, z.rem % K
        body = (NG - 1) * P * K

        @block.sync
        def _(eng):
            eng.wait_ge(cleared, 3)
            for n, a in enumerate((src, dst)):
                eng.dma_start(key[:, n, 0:T - K].rearrange("p (g k) -> p g k", k=K),
                              a[0:body].rearrange("(g p k) -> p g k", p=P, k=K)).then_inc(loaded, 16)
                if full:
                    eng.dma_start(key[0:full, n, T - K:T],
                                  a[body:body + full * K].rearrange("(p k) -> p k", k=K)).then_inc(loaded, 16)
                eng.dma_start(key[full:full + 1, n, T - K:T - K + tail],
                              a[body + full * K:z.E].rearrange("(o k) -> o k", o=1)).then_inc(loaded, 16)
            whole = z.N // P
            eng.dma_start(m["xn"][:, 0:whole, :], x[0:whole * P, :].rearrange("(b p) d -> p b d", p=P))\
               .then_inc(x_in, 16)
            if z.N % P:
                eng.dma_start(m["xn"][0:z.N % P, whole, :], x[whole * P:z.N, :]).then_inc(x_in, 16)
            eng.wait_ge(blk_ready, 1)
            eng.dma_start(m["blk"].rearrange("n (p c) -> p n c", c=z.UC), blki[:, :, :]).then_inc(blk_out, 16)
            eng.wait_ge(blk_out, 16)
            eng.dma_start(m["blkS"][0:1, :, :], m["blk"].rearrange("(o n) c -> o n c", o=1)).then_inc(blk_out, 16)
            eng.wait_ge(blk_out, 32)
            eng.wait_ge(x_in, 32 if z.N % P else 16)

        @block.scalar
        def _(eng):
            eng.wait_ge(cleared, 5)
            rows = m["rows"].rearrange("(p t) c -> p t c", p=P)
            assert z.TT % 8 == 0
            for t in range(0, z.TT, 8):
                eng.dma_start(rows[:, t:t + 8, :], fill[:, :, :]).then_inc(filled, 16)
            eng.dma_start(m["rows_d"].rearrange("(p t) c -> p t c", p=P), filld[:, :, :]).then_inc(filled, 16)
            eng.wait_ge(filled, 16 * (z.TT // 8 + 1))

        @block.gpsimd
        def _(eng):
            eng.memset(key[:, :, :], NB * P).then_inc(cleared, 1)
            eng.memset(m["xn"][:, :, :], 0.0).then_inc(cleared, 1)
            eng.memset(zer[:, :], 0.0).then_inc(cleared, 1)
            eng.memset(fill[:, :, :], 0.0).then_inc(made, 1)
            eng.memset(filld[:, :, :], 0.0).then_inc(made, 1)
            eng.wait_ge(made, 2)
            eng.memset(fill[:, :, D:D + 1], -1.0).then_inc(cleared, 1)
            eng.memset(filld[:, :, 1:2], -1.0).then_inc(cleared, 1)
            eng.iota(m["io50"][:, :], [[1, HB]], base=0, channel_multiplier=0,
                     allow_small_or_imprecise_dtypes=True).then_inc(made, 1)
            eng.iota(m["io128"][:, :], [[1, P]], base=0, channel_multiplier=0,
                     allow_small_or_imprecise_dtypes=True).then_inc(made, 1)
            eng.iota(m["io128b"][:, :], [[1, P]], base=0, channel_multiplier=0,
                     allow_small_or_imprecise_dtypes=True).then_inc(made, 1)
            eng.iota(m["pidx"][:, :], [[1, 1]], base=0, channel_multiplier=1,
                     allow_small_or_imprecise_dtypes=True).then_inc(made, 1)
            eng.iota(uidx[:, :], [[1, z.UC]], base=0, channel_multiplier=z.UC,
                     allow_small_or_imprecise_dtypes=True).then_inc(made, 1)
            eng.memset(m["onesb"][:, :], 1.0).then_inc(made, 1)
            eng.memset(m["onesf"][:, :], 1.0).then_inc(made, 1)

        @block.vector
        def _(eng):
            eng.wait_ge(made, 9)
            c = Count()
            eng.tensor_scalar(m["ident"][:, :], m["io128"][:, :], m["pidx"][:, 0:1], None,
                              ALU.is_equal).then_inc(v, c.up() and 1)
            eng.tensor_scalar(m["identb"][:, :], m["io128"][:, :], m["pidx"][:, 0:1], None,
                              ALU.is_equal).then_inc(v, c.up() and 1)
            eng.tensor_scalar(m["tri"][:, :], m["io128"][:, :], m["pidx"][:, 0:1], None,
                              ALU.is_gt).then_inc(v, c.up() and 1)
            eng.wait_ge(loaded, 16 * 2 * (3 if full else 2))
            eng.tensor_scalar(tmp[:, :, :], key[:, :, :], 7, None, ALU.arith_shift_right).then_inc(v, c.up() and 1)
            eng.wait_ge(v, c.n)
            eng.tensor_copy(m["hib"][:, :, :], tmp[:, :, :]).then_inc(v, c.up() and 1)
            eng.wait_ge(v, c.n)
            eng.tensor_scalar(tmp[:, :, :], key[:, :, :], P - 1, None, ALU.bitwise_and).then_inc(v, c.up() and 1)
            eng.tensor_scalar(neg[:, :, :], key[:, :, :], float(NB * P), float(-P), ALU.is_ge,
                              ALU.mult).then_inc(v, c.up() and 1)
            for n in range(2):
                eng.tensor_scalar(m["val"][:, 1 - n, :], key[:, n, :], float(z.N - 1), None,
                                  ALU.min).then_inc(v, c.up() and 1)
            eng.wait_ge(v, c.n)
            eng.tensor_tensor(m["lo"][:, :, :], tmp[:, :, :], neg[:, :, :], ALU.add).then_inc(v, c.up() and 1)
            eng.wait_ge(v, c.n)
            eng.tensor_copy(m["lob"][:, :], m["lo"][:, 1, :]).then_inc(v, c.up() and 1)
            eng.wait_ge(v, c.n)
            with eng.Fori(0, NG // 2) as i:
                for j in range(2):
                    eng.wait_ge(oh_used[j], i * 2)
                    for n in range(2):
                        eng.tensor_tensor(
                            oh[j][:, n, :].rearrange("p (k h) -> p k h", h=HB),
                            m["io50"][:, None, :].to_broadcast([P, K, HB]),
                            m["hib"][:, n, bass.ds((2 * i + j) * K, K)][:, :, None].to_broadcast([P, K, HB]),
                            ALU.is_equal).then_inc(oh_ready[j], 1)
            eng.wait_ge(counted, 1)
            for n in range(2):
                eng.tensor_reduce(cnt[:, n, :], psc[n][:, 0:K * HB].rearrange("p (k h) -> p h k", h=HB),
                                  AX.X, ALU.add).then_inc(v, c.up() and 1)
            eng.wait_ge(v, c.n)
            eng.tensor_scalar(cnti[:, :, :], cnt[:, :, :], float(P * UT - 1), None, ALU.add).then_inc(v, c.up() and 1)
            eng.wait_ge(v, c.n)
            eng.tensor_scalar(cnti[:, :, :], cnti[:, :, :], 8, None, ALU.arith_shift_right).then_inc(v, c.up() and 1)
            eng.wait_ge(v, c.n)
            eng.tensor_copy(uni[:, :, :], cnti[:, :, :]).then_inc(v, c.up() and 1)
            eng.wait_ge(v, c.n)
            for n in range(2):
                eng.tensor_tensor_scan(incl[:, n, :], m["onesf"][:, 0:HB], uni[:, n, :], 0.0, ALU.mult,
                                       ALU.add).then_inc(v, c.up() and 1)
            eng.wait_ge(v, c.n)
            eng.tensor_tensor(cnt[:, :, :], incl[:, :, :], uni[:, :, :], ALU.subtract).then_inc(v, c.up() and 1)
            eng.wait_ge(v, c.n)
            eng.tensor_scalar(m["base"][:, :, :], cnt[:, :, :], float(P * UT), None, ALU.mult).then_inc(v, c.up() and 1)
            for n in range(2):
                eng.tensor_tensor(cmp[:, n, :, :], uidx[:, :, None].to_broadcast([P, z.UC, HB]),
                                  incl[:, n, None, :].to_broadcast([P, z.UC, HB]), ALU.is_ge).then_inc(v, c.up() and 1)
            eng.wait_ge(v, c.n)
            for n in range(2):
                eng.tensor_reduce(blkf[:, n, :], cmp[:, n, :, :], AX.X, ALU.add).then_inc(v, c.up() and 1)
            eng.wait_ge(v, c.n)
            eng.tensor_scalar(blki[:, :, :], blkf[:, :, :], float(NB), None, ALU.min).then_inc(blk_ready, 1)

        @block.tensor
        def _(eng):
            eng.wait_ge(cleared, 3)
            eng.wait_ge(made, 9)
            for n in range(2):
                eng.matmul(psc[n][:, 0:K * HB], m["onesb"][:, :], zer[:, :], start=True, stop=False,
                           skip_group_check=True)
            with eng.Fori(0, NG // 2) as i:
                for j in range(2):
                    eng.wait_ge(oh_ready[j], i * 2 + 2)
                    for n in range(2):
                        eng.matmul(psc[n][:, 0:K * HB], m["onesb"][:, :], oh[j][:, n, :], start=False,
                                   stop=False, skip_group_check=True).then_inc(oh_used[j], 1)
            for n in range(2):
                mm = eng.matmul(psc[n][:, 0:K * HB], m["onesb"][:, :], zer[:, :], start=False, stop=True,
                                skip_group_check=True)
            mm.then_inc(counted, 1)


def sort_stage(nc, z, m, sb, ps, sem, ea):
    HB, NG = z.HB, z.NG
    with ExitStack() as ctx:
        rows = [sb(ctx, f"rowS{j}", [P, K, D + 2], fp32) for j in range(2)]
        rowd = [sb(ctx, f"rowD{j}", [P, K, 2], fp32) for j in range(2)]
        oh = [sb(ctx, f"ohr{j}", [P, 2, K + 1, HB], bf16) for j in range(2)]
        ohlo = [sb(ctx, f"ohlo{j}", [P, K, P], bf16) for j in range(2)]
        ranks = sb(ctx, "ranks", [P, 2, K, HB], fp32)
        posf = sb(ctx, "posf", [P, 2 * K], fp32)
        posi = sb(ctx, "posi", [P, 2 * K], i32)
        lane = sb(ctx, "lane", [P, 2 * K], i32)
        tile = sb(ctx, "tile", [P, 2 * K], i32)
        idx = [sb(ctx, f"idx{j}", [P, 2 * K], i32) for j in range(2)]
        psr = [[ps(ctx, f"psr{j}{n}", [P, 512], fp32) for n in range(2)] for j in range(2)]
        psd = ps(ctx, "psd", [P, 512], fp32)
        cleared = sem(ctx, "ohpad")
        ea_in = [sem(ctx, f"ea_in{j}") for j in range(2)]
        sent_s = [sem(ctx, f"sent_s{j}") for j in range(2)]
        sent_d = [sem(ctx, f"sent_d{j}") for j in range(2)]
        oh_ready = [sem(ctx, f"ohr_ready{j}") for j in range(2)]
        ranked = [sem(ctx, f"ranked{j}") for j in range(2)]
        summed = [sem(ctx, f"summed{j}") for j in range(2)]
        degs = [sem(ctx, f"degs{j}") for j in range(2)]
        idx_ready = [sem(ctx, f"idx_ready{j}") for j in range(2)]
        v = sem(ctx, "v_sort")
        deg_ready = sem(ctx, "deg_ready")
        begun = sem(ctx, "scatter_begun")
        block = ctx.enter_context(nc.Block())
        full, tail = z.rem // K, z.rem % K
        ea_g = ea[0:(NG - 1) * P * K, :].rearrange("(g p k) d -> g p k d", p=P, k=K)
        last = ea[(NG - 1) * P * K:z.E, :]

        @block.sync
        def _(eng):
            def load(i, j):
                eng.wait_ge(sent_s[j], i * 16 * K)
                if isinstance(i, int) and 2 * i + j == NG - 1:
                    if full:
                        eng.dma_start(rows[j][0:full, :, 0:D], last[0:full * K, :].rearrange("(p k) d -> p k d", k=K))\
                           .then_inc(ea_in[j], 16)
                    eng.dma_start(rows[j][full:full + 1, 0:tail, 0:D],
                                  last[full * K:, :].rearrange("(p k) d -> p k d", p=1)).then_inc(ea_in[j], 16)
                else:
                    g = 2 * i + j
                    a = ea_g[g] if isinstance(g, int) else ea_g[bass.ds(g, 1)].rearrange("o p k d -> (o p) k d")
                    eng.dma_start(rows[j][:, :, 0:D], a).then_inc(ea_in[j], 16)

            with eng.Fori(0, NG // 2 - 1) as i:
                for j in range(2):
                    load(i, j)
            for j in range(2):
                load(NG // 2 - 1, j)

        @block.gpsimd
        def _(eng):
            def scatter(i, j, arrived):
                eng.wait_ge(ea_in[j], arrived)
                eng.wait_ge(idx_ready[j], i + 1)
                eng.sem_inc(begun, 1)
                for k in range(K):
                    eng.indirect_dma_start(
                        out=m["rows"], out_offset=bass.IndirectOffsetOnAxis(ap=idx[j][:, k:k + 1], axis=0),
                        in_=rows[j][:, k, :], in_offset=None).then_inc(sent_s[j], 16)
                    eng.indirect_dma_start(
                        out=m["rows_d"], out_offset=bass.IndirectOffsetOnAxis(ap=idx[j][:, K + k:K + k + 1], axis=0),
                        in_=rowd[j][:, k, :], in_offset=None).then_inc(sent_d[j], 16)

            with eng.Fori(0, NG // 2 - 1) as i:
                for j in range(2):
                    scatter(i, j, (i + 1) * 16)
            for j in range(2):
                scatter(NG // 2 - 1, j, NG // 2 * 16 + (16 if j == 1 and full else 0))
            for j in range(2):
                eng.wait_ge(sent_s[j], NG // 2 * 16 * K)
                eng.wait_ge(sent_d[j], NG // 2 * 16 * K)

        @block.vector
        def _(eng):
            for j in range(2):
                eng.memset(oh[j][:, :, K, :], 0.0).then_inc(cleared, 1)
            with eng.Fori(0, NG // 2) as i:
                for j in range(2):
                    g = (2 * i + j) * K
                    step = Count()

                    def own():
                        return i * 20 + j * 10 + step.n

                    eng.wait_ge(ranked[j], i)
                    eng.wait_ge(degs[j], i)
                    for n in range(2):
                        eng.tensor_tensor(
                            oh[j][:, n, 0:K, :], m["io50"][:, None, :].to_broadcast([P, K, HB]),
                            m["hib"][:, n, bass.ds(g, K)][:, :, None].to_broadcast([P, K, HB]),
                            ALU.is_equal).then_inc(oh_ready[j], 1)
                    eng.tensor_tensor(
                        ohlo[j][:, :, :], m["io128b"][:, None, :].to_broadcast([P, K, P]),
                        m["lob"][:, bass.ds(g, K)][:, :, None].to_broadcast([P, K, P]),
                        ALU.is_equal).then_inc(oh_ready[j], 1)
                    eng.wait_ge(sent_s[j], i * 16 * K)
                    eng.wait_ge(sent_d[j], i * 16 * K)
                    eng.tensor_copy(rows[j][:, :, D], m["lo"][:, 0, bass.ds(g, K)])
                    eng.tensor_copy(rows[j][:, :, D + 1].bitcast(i32), m["val"][:, 0, bass.ds(g, K)])
                    eng.tensor_copy(rowd[j][:, :, 0].bitcast(i32), m["val"][:, 1, bass.ds(g, K)])
                    eng.tensor_copy(rowd[j][:, :, 1], m["lo"][:, 1, bass.ds(g, K)])
                    eng.wait_ge(ranked[j], i + 1)
                    for n in range(2):
                        eng.tensor_tensor(
                            ranks[:, n, :, :], psr[j][n][:, 0:K * HB].rearrange("p (k h) -> p k h", h=HB),
                            m["base"][:, n, None, :].to_broadcast([P, K, HB]), ALU.add).then_inc(v, step.up() and 1)
                    eng.wait_ge(v, own())
                    for n in range(2):
                        eng.tensor_tensor(m["base"][:, n, :], m["base"][:, n, :],
                                          psr[j][n][:, K * HB:(K + 1) * HB], ALU.add).then_inc(summed[j], 1)
                    eng.tensor_tensor(ranks[:, :, :, :], ranks[:, :, :, :], oh[j][:, :, 0:K, :],
                                      ALU.mult).then_inc(v, step.up() and 1)
                    eng.wait_ge(v, own())
                    eng.tensor_reduce(posf[:, :], ranks[:, :, :, :].rearrange("p n k h -> p (n k) h"),
                                      AX.X, ALU.add).then_inc(v, step.up() and 1)
                    eng.wait_ge(v, own())
                    eng.tensor_copy(posi[:, :], posf[:, :]).then_inc(v, step.up() and 1)
                    eng.wait_ge(v, own())
                    eng.tensor_scalar(lane[:, :], posi[:, :], P - 1, None, ALU.bitwise_and).then_inc(v, step.up() and 1)
                    eng.tensor_scalar(tile[:, :], posi[:, :], 7, None, ALU.arith_shift_right).then_inc(v, step.up() and 1)
                    eng.wait_ge(v, own())
                    eng.scalar_tensor_tensor(idx[j][:, :], lane[:, :], float(z.TT), tile[:, :], ALU.mult,
                                             ALU.add).then_inc(idx_ready[j], 1)
                    while step.n < 10:
                        eng.sem_inc(v, 1)
                        step.up()
            eng.wait_ge(deg_ready, 1)
            eng.tensor_copy(m["deg"][:, :], psd[:, 0:z.NB])

        @block.tensor
        def _(eng):
            eng.wait_ge(cleared, 2)
            eng.matmul(psd[:, 0:HB], m["onesb"][:, :], oh[0][:, 0, K, :], start=True, stop=False,
                       skip_group_check=True)
            with eng.Fori(0, NG // 2) as i:
                for j in range(2):
                    eng.wait_ge(oh_ready[j], (i + 1) * 3)
                    eng.wait_ge(summed[j], i * 2)
                    for n in range(2):
                        eng.matmul(psr[j][n][:, 0:(K + 1) * HB], m["tri"][:, :],
                                   oh[j][:, n, :, :].rearrange("p k h -> p (k h)"), start=True, stop=False,
                                   skip_group_check=True)
                        for d in range(1, K + 1):
                            mm = eng.matmul(psr[j][n][:, d * HB:(K + 1) * HB], m["onesb"][:, :],
                                            oh[j][:, n, 0:K + 1 - d, :].rearrange("p k h -> p (k h)"),
                                            start=False, stop=(d == K), skip_group_check=True)
                    mm.then_inc(ranked[j], 1)
                    for k in range(K):
                        mm = eng.matmul(psd[:, 0:HB], ohlo[j][:, k, :], oh[j][:, 1, k, :], start=False,
                                        stop=False, skip_group_check=True)
                    mm.then_inc(degs[j], 1)
            eng.matmul(psd[:, 0:HB], m["onesb"][:, :], oh[0][:, 0, K, :], start=False, stop=True,
                       skip_group_check=True).then_inc(deg_ready, 1)


def chunk_transform(nc, z, ctx, sb, ps, sem, m, name, source, w_sb, w_dma, cols, finish, tail=None):
    xc = [sb(ctx, f"{name}_xc", [P, BC, D], fp32)]
    xT = sb(ctx, f"{name}_xT", [D, BC * P], fp32)
    psT = [ps(ctx, f"{name}_psT{n}", [P, 512], fp32) for n in range(2)]
    nb = -(-BC * cols // 512)
    psW = [ps(ctx, f"{name}_psW{n}", [P, 512], fp32) for n in range(nb)]
    per = 512 // cols
    copied, turned, turned_sb, times, finished, w_in, begun = (
        sem(ctx, f"{name}_{s}") for s in ("copied", "turned", "evac", "times", "finished", "w_in", "begun"))
    block = ctx.enter_context(nc.Block())
    first = 4
    n_it = z.NB // BC

    @block.sync
    def _(eng):
        w_dma(eng, w_in)
        if tail:
            tail(eng, finished, n_it)

    @block.scalar
    def _(eng):
        with eng.Fori(0, n_it) as i:
            eng.wait_ge(turned, i)
            eng.activation(xc[0][:, :, :].rearrange("p b d -> p (b d)"),
                           source[:, :, :].rearrange("p b d -> p (b d)")[:, bass.ds(i * BC * D, BC * D)],
                           ACT.Copy).then_inc(copied, 1)
            eng.wait_ge(turned, i + 1)
            eng.wait_ge(times, i)
            eng.activation(xT[:, 0:first * P], psT[0][0:D, 0:first * P], ACT.Copy)
            eng.activation(xT[:, first * P:BC * P], psT[1][0:D, 0:(BC - first) * P], ACT.Copy).then_inc(turned_sb, 1)

    @block.tensor
    def _(eng):
        eng.wait_ge(w_in, 16)
        with eng.Fori(0, n_it) as i:
            eng.wait_ge(copied, i + 1)
            eng.wait_ge(turned_sb, i)
            eng.sem_inc(begun, 1)
            for b in range(BC):
                q = 0 if b < first else 1
                o = (b - (first if q else 0)) * P
                mm = eng.transpose(psT[q][0:D, o:o + P], xc[0][:, b, :], m["ident"][:, :])
            mm.then_inc(turned, 1)
            eng.wait_ge(turned_sb, i + 1)
            eng.wait_ge(finished, i)
            for b in range(BC):
                mm = eng.matmul(psW[b // per][:, b % per * cols:(b % per + 1) * cols], xT[:, b * P:(b + 1) * P],
                                w_sb, start=True, stop=True)
            mm.then_inc(times, 1)

    @block.vector
    def _(eng):
        with eng.Fori(0, n_it) as i:
            eng.wait_ge(times, i + 1)
            finish(eng, i, psW, finished)


def table_stage(nc, z, m, sb, ps, sem, W):
    with ExitStack() as ctx:
        part = sb(ctx, "part", [P, BC * C], fp32)
        v = sem(ctx, "v_tab")
        per = 512 // C * C

        def finish(eng, i, psW, finished):
            def cols(n, q, w):
                return m["P3"][n][:, bass.ds(i * (BC * C) + q * per, w)]

            widths = [min(per, BC * C - q * per) for q in range(len(psW))]
            nq = len(psW)
            for q, w in enumerate(widths):
                eng.tensor_copy(cols(0, q, w), psW[q][:, 0:w]).then_inc(v, 1)
            eng.wait_ge(v, i * 4 * nq + nq)
            for q, w in enumerate(widths):
                ins = eng.tensor_tensor(part[:, q * per:q * per + w], psW[q][:, 0:w], cols(0, q, w), ALU.subtract)
                ins.then_inc(v, 1)
            eng.wait_ge(v, i * 4 * nq + 2 * nq)
            for q, w in enumerate(widths):
                eng.tensor_copy(cols(1, q, w), part[:, q * per:q * per + w]).then_inc(v, 1)
            eng.wait_ge(v, i * 4 * nq + 3 * nq)
            for q, w in enumerate(widths):
                eng.tensor_tensor(part[:, q * per:q * per + w], part[:, q * per:q * per + w], cols(1, q, w),
                                  ALU.subtract).then_inc(v, 1)
            eng.wait_ge(v, i * 4 * nq + 4 * nq)
            for q, w in enumerate(widths):
                ins = eng.tensor_copy(cols(2, q, w), part[:, q * per:q * per + w])
            ins.then_inc(finished, 1)

        def w_dma(eng, w_in):
            eng.dma_start(m["Wsb"][:, :], W).then_inc(w_in, 16)

        chunk_transform(nc, z, ctx, sb, ps, sem, m, "tab", m["xn"], m["Wsb"][0:D, :], w_dma, C, finish)


def edge_stage(nc, z, m, sb, ps, sem, att):
    HB, NU = z.HB, z.NU
    n_it = NU // BU
    with ExitStack() as ctx:
        buf = [sb(ctx, f"buf{j}", [P, UT, 2 * D + 2], fp32) for j in range(BU)]
        one = [sb(ctx, f"one{q}", [P, UT, P], bf16) for q in range(2)]
        xeT = [sb(ctx, f"xeT{q}", [P, UT * P], fp32) for q in range(2)]
        oneT = [sb(ctx, f"oneT{q}", [P, UT * P], bf16) for q in range(2)]
        ex = [sb(ctx, f"ex{q}", [P, UT * 2 * C], fp32) for q in range(2)]
        lg = [sb(ctx, f"lg{q}", [P, UT * 2 * C], fp32) for q in range(2)]
        sp = [sb(ctx, f"sp{q}", [P, UT, 2, H, D], fp32) for q in range(2)]
        attb = sb(ctx, "attb", [P, 2, H, D], fp32)
        junk = [sb(ctx, f"junk{q}", [P, UT * H, 2, D], bf16) for q in range(2)]
        sums = sb(ctx, "sums", [P, BU * UT * H], fp32)
        psx = [ps(ctx, f"psx{q}", [P, 512], fp32) for q in range(2)]
        pso = [ps(ctx, f"pso{q}", [P, 1024], bf16) for q in range(2)]
        pre = [ps(ctx, f"pre{q}", [P, UT, 2, C], fp32) for q in range(2)]

        def sems(name, n=BU):
            return [sem(ctx, f"{name}{j}") for j in range(n)]

        row_in, got, lo_kept, one_ready, x_turned, o_turned, x_evac, o_evac, pre_ready, exp_done, ln_done, \
            sp_ready, sp_read, stored = (sems(s) for s in (
                "row_in", "got", "lo_kept", "one_ready", "x_turned", "o_turned", "x_evac", "o_evac",
                "pre_ready", "exp_done", "ln_done", "sp_ready", "sp_read", "stored"))
        att_in = sem(ctx, "att_in")
        padded = sem(ctx, "padded")
        begun = sem(ctx, "gather_begun")
        kept = sem(ctx, "sums_kept")
        block = ctx.enter_context(nc.Block())
        rows = m["rows"].rearrange("(p t) c -> p t c", p=P)

        def before(i, j):
            return (j - 2, i + 1) if j >= 2 else (j + 2, i)

        @block.sync
        def _(eng):
            for n in range(2):
                eng.dma_start(attb[:, n, :, :], att[:, :, n * D:(n + 1) * D].to_broadcast([P, H, D]))\
                   .then_inc(att_in, 16)
            with eng.Fori(0, n_it) as i:
                for j in range(BU):
                    eng.wait_ge(x_turned[j], i)
                    eng.wait_ge(lo_kept[j], i)
                    eng.dma_start(buf[j][:, :, D:2 * D + 2],
                                  rows[:, bass.ds((i * BU + j) * UT, UT), :]).then_inc(row_in[j], 16)

        @block.gpsimd
        def _(eng):
            for n in range(3):
                eng.memset(m["P3"][n][:, z.NB * C:HB * C], 0.0).then_inc(padded, 1)
            with eng.Fori(0, n_it) as i:
                for j in range(BU):
                    eng.wait_ge(row_in[j], (i + 1) * 16)
                    eng.sem_inc(begun, 1)
                    for k in range(UT):
                        eng.indirect_dma_start(
                            out=buf[j][:, k, 0:D], out_offset=None, in_=m["x_in"],
                            in_offset=bass.IndirectOffsetOnAxis(
                                ap=buf[j][:, k, 2 * D + 1:2 * D + 2].bitcast(i32), axis=0)).then_inc(got[j], 16)

        @block.vector
        def _(eng):
            def places(i, j):
                q = j % 2
                o, c = before(i, j)
                eng.wait_ge(row_in[j], (i + 1) * 16)
                eng.wait_ge(o_turned[o], c)
                for k in range(UT):
                    ins = eng.tensor_scalar(one[q][:, k, :], m["io128b"][:, :], buf[j][:, k, 2 * D:2 * D + 1],
                                            None, ALU.is_equal)
                ins.then_inc(one_ready[j], 1)
                eng.tensor_copy(m["loA"][:, bass.ds((i * BU + j) * UT, UT)] if not isinstance(i, int) else
                                m["loA"][:, (i * BU + j) * UT:(i * BU + j + 1) * UT],
                                buf[j][:, :, 2 * D]).then_inc(lo_kept[j], 1)

            def finish(i, j):
                q = j % 2
                o, c = before(i, j)
                eng.wait_ge(ln_done[j], i + 1)
                eng.wait_ge(stored[o], c * 16)
                eng.wait_ge(sp_read[o], c)
                eng.scalar_tensor_tensor(sp[q][:, :, :, :, :].rearrange("p k s h d -> p (k s h d)"),
                                         lg[q][:, :], CAP_SP,
                                         pre[q][:, :, :, :].rearrange("p k s c -> p (k s c)"),
                                         ALU.min, ALU.max).then_inc(sp_ready[j], 1)
                eng.wait_ge(sp_ready[j], i + 1)
                if j == 0:
                    eng.wait_ge(kept, i)
                for k in range(UT):
                    for h in range(H):
                        n = (j * UT + k) * H + h
                        ins = eng.tensor_tensor_reduce(junk[q][:, k * H + h, :, :], sp[q][:, k, :, h, :], attb[:, :, h, :],
                                                       1.0, 0.0, ALU.mult, ALU.add, sums[:, n:n + 1])
                ins.then_inc(sp_read[j], 1)

            def keep(i):
                eng.wait_ge(sp_read[BU - 1], i + 1)
                w = BU * UT
                eng.tensor_copy(m["alpha"][:, bass.ds(i * w, w) if not isinstance(i, int) else
                                           slice(i * w, i * w + w), :],
                                sums[:, :].rearrange("p (t h) -> p t h", h=H)).then_inc(kept, 1)

            eng.wait_ge(att_in, 32)
            places(0, 0)
            places(0, 1)
            with eng.Fori(0, n_it - 1) as i:
                for j in range(BU):
                    places(*seg(i, j + 2, BU))
                    finish(i, j)
                keep(i)
            for j in range(BU):
                if j + 2 < BU:
                    places(n_it - 1, j + 2)
                finish(n_it - 1, j)
            keep(n_it - 1)

        @block.scalar
        def _(eng):
            def evacuate(i, j):
                q = j % 2
                o, c = before(i, j)
                eng.wait_ge(pre_ready[o], c)
                eng.wait_ge(x_turned[j], i + 1)
                eng.activation(xeT[q][:, :], psx[q][:, 0:UT * P], ACT.Copy).then_inc(x_evac[j], 1)
                eng.wait_ge(o_turned[j], i + 1)
                eng.activation(oneT[q][:, :], pso[q][:, 0:UT * P], ACT.Copy).then_inc(o_evac[j], 1)

            def softplus(i, j):
                q = j % 2
                o, c = before(i, j)
                eng.wait_ge(pre_ready[j], i + 1)
                eng.wait_ge(ln_done[o], c)
                eng.activation(ex[q][:, :], pre[q][:, :, :, :].rearrange("p k s c -> p (k s c)"), ACT.Exp)\
                   .then_inc(exp_done[j], 1)
                eng.wait_ge(exp_done[j], i + 1)
                eng.wait_ge(sp_ready[o], c)
                eng.activation(lg[q][:, :], ex[q][:, :], ACT.Ln, bias=1.0).then_inc(ln_done[j], 1)

            def store(i, j):
                q = j % 2
                eng.wait_ge(sp_ready[j], i + 1)
                w = UT * C
                a = (i * BU + j) * w
                eng.dma_start(m["outj"][:, bass.ds(a, w) if not isinstance(i, int) else slice(a, a + w)]
                              .rearrange("p (k c) -> p k c", c=C),
                              sp[q][:, :, 1, :, :].rearrange("p k h d -> p k (h d)")).then_inc(stored[j], 16)

            evacuate(0, 0)
            evacuate(0, 1)
            softplus(0, 0)
            with eng.Fori(0, n_it - 1) as i:
                for j in range(BU):
                    evacuate(*seg(i, j + 2, BU))
                    softplus(*seg(i, j + 1, BU))
                    store(i, j)
            for j in range(BU):
                if j + 2 < BU:
                    evacuate(n_it - 1, j + 2)
                if j + 1 < BU:
                    softplus(n_it - 1, j + 1)
                store(n_it - 1, j)
            for j in range(BU):
                eng.wait_ge(stored[j], n_it * 16)

        @block.tensor
        def _(eng):
            def turn(i, j):
                q = j % 2
                o, c = before(i, j)
                eng.wait_ge(one_ready[j], i + 1)
                eng.wait_ge(o_evac[o], c)
                for k in range(UT):
                    mm = eng.transpose(pso[q][:, k * P:(k + 1) * P], one[q][:, k, :], m["identb"][:, :])
                mm.then_inc(o_turned[j], 1)
                eng.wait_ge(got[j], (i + 1) * 16 * UT)
                eng.wait_ge(x_evac[o], c)
                for k in range(UT):
                    mm = eng.transpose(psx[q][:, k * P:(k + 1) * P], buf[j][:, k, 0:2 * D], m["ident"][:, :])
                mm.then_inc(x_turned[j], 1)

            def product(i, j, b):
                q = j % 2
                o, c = before(i, j)
                eng.wait_ge(x_evac[j], i + 1)
                eng.wait_ge(o_evac[j], i + 1)
                eng.wait_ge(sp_ready[o], c)
                for k in range(UT):
                    xt = xeT[q][:, k * P:(k + 1) * P]
                    eng.matmul(pre[q][:, k, 1, :], xt, m["Wsb"][:, :], start=True, stop=True)
                    eng.matmul(pre[q][:, k, 0, :], xt[D:2 * D, :], m["Wsb"][D:2 * D, :], start=True, stop=False,
                               skip_group_check=True)
                    for n in range(3):
                        mm = eng.matmul(pre[q][:, k, 0, :], oneT[q][:, k * P:(k + 1) * P],
                                        m["P3"][n][:, bass.ds(b * C, C)], start=False, stop=(n == 2),
                                        skip_group_check=True)
                mm.then_inc(pre_ready[j], 1)

            def block_of(i, j):
                u = i * BU + j
                return eng.value_load(m["blkS"][0:1, 0, bass.ds(u, 1) if not isinstance(i, int) else slice(u, u + 1)],
                                      min_val=0, max_val=HB - 1)

            eng.wait_ge(padded, 3)
            turn(0, 0)
            with eng.Fori(0, n_it - 1) as i:
                for j in range(BU):
                    b = block_of(i, j)
                    turn(*seg(i, j + 1, BU))
                    product(i, j, b)
            for j in range(BU):
                b = block_of(n_it - 1, j)
                if j + 1 < BU:
                    turn(n_it - 1, j + 1)
                product(n_it - 1, j, b)


def newton_rsqrt(eng, v, c, a, y, t):
    eng.tensor_tensor(t, y, y, ALU.mult).then_inc(v, c.up() and 1)
    eng.wait_ge(v, c.n)
    eng.tensor_tensor(t, t, a, ALU.mult).then_inc(v, c.up() and 1)
    eng.wait_ge(v, c.n)
    eng.tensor_scalar(t, t, -0.5, 1.5, ALU.mult, ALU.add).then_inc(v, c.up() and 1)
    eng.wait_ge(v, c.n)
    eng.tensor_tensor(y, y, t, ALU.mult).then_inc(v, c.up() and 1)
    eng.wait_ge(v, c.n)


def softmax_stage(nc, z, m, sb, ps, sem, gamma, beta):
    TT = z.TT
    A = m["alpha"]
    with ExitStack() as ctx:
        t1 = sb(ctx, "t1", [P, TT, H], fp32)
        mask = sb(ctx, "mask", [P, TT], fp32)
        msum = sb(ctx, "msum", [P, H], fp32)
        mu = sb(ctx, "mu", [P, H], fp32)
        sq = sb(ctx, "sq", [P, H], fp32)
        var = sb(ctx, "var", [P, H], fp32)
        rs = sb(ctx, "rs", [P, H], fp32)
        tt = sb(ctx, "tt", [P, H], fp32)
        pmax = sb(ctx, "pmax", [P, H], fp32)
        gmax = sb(ctx, "gmax", [H, 1], fp32)
        dg = sb(ctx, "dg", [H, H], fp32)
        top = sb(ctx, "top", [P, H], fp32)
        gb = sb(ctx, "gb", [P, 2, H], fp32)
        psS = [ps(ctx, f"psS{n}", [P, 512], fp32) for n in range(4)]
        v = sem(ctx, "v_sm")
        ln_ready = sem(ctx, "sm_ln")
        exp_done = sem(ctx, "sm_exp")
        par_in = sem(ctx, "par_in")
        sums_ready, squares_ready, var_ready, root_ready, normed, maxima, diag, shifted = (
            sem(ctx, f"sm_{s}") for s in ("sums", "squares", "var", "root", "normed", "maxima", "diag", "shifted"))
        across = sem(ctx, "sm_across")
        block = ctx.enter_context(nc.Block())

        def flat(t):
            return t[:, :, :].rearrange("p t h -> p (t h)")

        def by_head(t):
            return t[:, :, :].rearrange("p t h -> p h t")

        def all_tiles(x):
            return x[:, None, :].to_broadcast([P, TT, H])

        maskb = mask[:, :, None].to_broadcast([P, TT, H])

        @block.sync
        def _(eng):
            for n, g in enumerate((gamma, beta)):
                eng.dma_start(gb[:, n, :], g.rearrange("(o h) -> o h", o=1).to_broadcast([P, H])).then_inc(par_in, 16)

        @block.scalar
        def _(eng):
            eng.activation(flat(t1), flat(A), ACT.Exp).then_inc(exp_done, 1)
            eng.wait_ge(exp_done, 1)
            eng.activation(flat(t1), flat(t1), ACT.Ln, bias=1.0).then_inc(ln_ready, 1)
            eng.wait_ge(var_ready, 1)
            eng.activation(rs[:, :], var[:, :], ACT.Sqrt).then_inc(root_ready, 1)
            eng.wait_ge(normed, 1)
            eng.activation(flat(t1), flat(A), ACT.Exp).then_inc(exp_done, 1)
            eng.wait_ge(exp_done, 2)
            eng.activation(flat(t1), flat(t1), ACT.Ln, bias=1.0).then_inc(ln_ready, 1)
            eng.wait_ge(shifted, 1)
            eng.activation(flat(t1), flat(A), ACT.Exp).then_inc(exp_done, 1)

        @block.tensor
        def _(eng):
            eng.wait_ge(sums_ready, 1)
            eng.matmul(psS[0][:, 0:H], m["onesf"][:, :], msum[:, :], start=True, stop=True).then_inc(across, 1)
            eng.wait_ge(squares_ready, 1)
            eng.matmul(psS[1][:, 0:H], m["onesf"][:, :], sq[:, :], start=True, stop=True).then_inc(across, 1)
            eng.wait_ge(maxima, 1)
            eng.transpose(psS[2][0:H, 0:P], pmax[:, :], m["ident"][:, :]).then_inc(across, 1)
            eng.wait_ge(diag, 1)
            eng.matmul(psS[3][:, 0:H], m["onesf"][0:H, :], dg[:, :], start=True, stop=True).then_inc(across, 1)

        @block.vector
        def _(eng):
            c = Count()

            def done(ins):
                ins.then_inc(v, c.up() and 1)
                eng.wait_ge(v, c.n)

            done(eng.tensor_scalar(mask[:, :], m["loA"][:, :], 0.0, None, ALU.is_ge))
            eng.wait_ge(ln_ready, 1)
            done(eng.scalar_tensor_tensor(flat(A), flat(t1), CAP_SP, flat(A), ALU.min, ALU.max))
            done(eng.tensor_tensor(t1[:, :, :], A[:, :, :], maskb, ALU.mult))
            eng.tensor_reduce(msum[:, :], by_head(t1), AX.X, ALU.add).then_inc(sums_ready, 1)
            eng.wait_ge(across, 1)
            done(eng.tensor_scalar(mu[:, :], psS[0][:, 0:H], 1.0 / z.E, None, ALU.mult))
            done(eng.tensor_tensor(A[:, :, :], A[:, :, :], all_tiles(mu), ALU.subtract))
            done(eng.tensor_tensor(t1[:, :, :], A[:, :, :], maskb, ALU.mult))
            done(eng.tensor_tensor(t1[:, :, :], t1[:, :, :], A[:, :, :], ALU.mult))
            eng.tensor_reduce(sq[:, :], by_head(t1), AX.X, ALU.add).then_inc(squares_ready, 1)
            eng.wait_ge(across, 2)
            eng.tensor_scalar(var[:, :], psS[1][:, 0:H], 1.0 / z.E, BN_EPS, ALU.mult, ALU.add).then_inc(var_ready, 1)
            eng.wait_ge(root_ready, 1)
            done(eng.reciprocal(rs[:, :], rs[:, :]))
            newton_rsqrt(eng, v, c, var[:, :], rs[:, :], tt[:, :])
            eng.wait_ge(par_in, 32)
            done(eng.tensor_tensor(rs[:, :], rs[:, :], gb[:, 0, :], ALU.mult))
            done(eng.tensor_tensor(A[:, :, :], A[:, :, :], all_tiles(rs), ALU.mult))
            eng.tensor_tensor(A[:, :, :], A[:, :, :], gb[:, 1, None, :].to_broadcast([P, TT, H]), ALU.add)\
               .then_inc(normed, 1)
            eng.wait_ge(ln_ready, 2)
            done(eng.scalar_tensor_tensor(flat(A), flat(t1), CAP_SP, flat(A), ALU.min, ALU.max))
            done(eng.tensor_tensor(A[:, :, :], A[:, :, :], maskb, ALU.mult))
            eng.tensor_reduce(pmax[:, :], by_head(A), AX.X, ALU.max).then_inc(maxima, 1)
            eng.wait_ge(across, 3)
            done(eng.tensor_reduce(gmax[:, :], psS[2][0:H, 0:P], AX.X, ALU.max))
            eng.tensor_scalar(dg[:, :], m["ident"][0:H, 0:H], gmax[:, 0:1], None, ALU.mult).then_inc(diag, 1)
            eng.wait_ge(across, 4)
            done(eng.tensor_copy(top[:, :], psS[3][:, 0:H]))
            eng.tensor_tensor(A[:, :, :], A[:, :, :], all_tiles(top), ALU.subtract).then_inc(shifted, 1)
            eng.wait_ge(exp_done, 3)
            done(eng.tensor_tensor(A[:, :, :], t1[:, :, :], maskb, ALU.mult))


def message_stage(nc, z, m, sb, ps, sem):
    n_it = z.NU // BU
    with ExitStack() as ctx:
        oj = [sb(ctx, f"oj{j}", [P, UT, H, D], fp32) for j in range(BU)]
        msg = [sb(ctx, f"msg{q}", [P, UT, C + H], fp32) for q in range(2)]
        one = [sb(ctx, f"onem{q}", [P, UT, P], fp32) for q in range(2)]
        psm = [ps(ctx, f"psm{q}", [P, 512], fp32) for q in range(4)]
        oj_in, oj_used, msg_ready, summed, added = ([sem(ctx, f"{s}{j}") for j in range(BU)] for s in (
            "oj_in", "oj_used", "msg_ready", "msg_summed", "msg_added"))
        cleared = sem(ctx, "acc_zero")
        block = ctx.enter_context(nc.Block())

        @block.sync
        def _(eng):
            with eng.Fori(0, n_it) as i:
                for j in range(BU):
                    eng.wait_ge(oj_used[j], i)
                    eng.dma_start(oj[j][:, :, :, :].rearrange("p k h d -> p (k h d)"),
                                  m["outj"][:, bass.ds((i * BU + j) * UT * C, UT * C)]).then_inc(oj_in[j], 16)

        @block.gpsimd
        def _(eng):
            eng.memset(m["acc"][:, :, :], 0.0).then_inc(cleared, 1)

        @block.vector
        def _(eng):
            def product(i, j, r):
                q = j % 2
                o, c = (j - 2, i + 1) if j >= 2 else (j + 2, i)
                t = (i * BU + j) * UT
                eng.wait_ge(oj_in[j], (i + 1) * 16)
                eng.wait_ge(summed[o], c)
                eng.tensor_tensor(msg[q][:, :, 0:C].rearrange("p k (h d) -> p k h d", h=H), oj[j][:, :, :, :],
                                  m["alpha"][:, r(t, UT), :][:, :, :, None].to_broadcast([P, UT, H, D]),
                                  ALU.mult).then_inc(oj_used[j], 1)
                eng.tensor_copy(msg[q][:, :, C:C + H], m["alpha"][:, r(t, UT), :]).then_inc(msg_ready[j], 1)
                for k in range(UT):
                    eng.tensor_scalar(one[q][:, k, :], m["io128"][:, :], m["loA"][:, r(t + k, 1)], None,
                                      ALU.is_equal).then_inc(msg_ready[j], 1)

            def add(i, j):
                u = i * BU + j
                src_ = m["blkS"][0:1, 0, bass.ds(u, 1) if not isinstance(i, int) else slice(u, u + 1)]
                b = eng.value_load(src_, min_val=0, max_val=z.HB - 1)
                eng.wait_ge(summed[j], i + 1)
                if j == 0:
                    eng.wait_ge(added[BU - 1], i)
                else:
                    eng.wait_ge(added[j - 1], i + 1)
                a = m["acc"][:, bass.ds(b, 1), :].rearrange("p o c -> p (o c)")
                eng.tensor_tensor(a, a, psm[j][:, 0:C + H], ALU.add).then_inc(added[j], 1)

            def dyn(a, w):
                return bass.ds(a, w)

            def fixed(a, w):
                return slice(a, a + w)

            eng.wait_ge(cleared, 1)
            product(0, 0, fixed)
            with eng.Fori(0, n_it - 1) as i:
                for j in range(BU):
                    product(*seg(i, j + 1, BU), dyn)
                    add(i, j)
            for j in range(BU):
                if j + 1 < BU:
                    product(n_it - 1, j + 1, fixed)
                add(n_it - 1, j)

        @block.tensor
        def _(eng):
            with eng.Fori(0, n_it) as i:
                for j in range(BU):
                    q = j % 2
                    eng.wait_ge(msg_ready[j], (i + 1) * (1 + UT))
                    eng.wait_ge(added[j], i)
                    for k in range(UT):
                        mm = eng.matmul(psm[j][:, 0:C + H], one[q][:, k, :], msg[q][:, k, :], start=(k == 0),
                                        stop=(k == UT - 1))
                    mm.then_inc(summed[j], 1)


class Norm:

    def __init__(self, z, ctx, sb, sem, name):
        self.z = z
        self.d2 = sb(ctx, f"{name}_d2", [P, z.NB, D], fp32)
        self.mean, self.var, self.rs, self.tt = (
            sb(ctx, f"{name}_{s}", [P, z.NB], fp32) for s in ("mean", "var", "rs", "tt"))
        self.var_ready, self.root_ready = sem(ctx, f"{name}_var"), sem(ctx, f"{name}_root")

    def scalar(self, eng):
        eng.wait_ge(self.var_ready, 1)
        eng.activation(self.rs[:, :], self.var[:, :], ACT.Sqrt).then_inc(self.root_ready, 1)

    def vector(self, eng, a, out, v, c):
        def done(ins):
            ins.then_inc(v, c.up() and 1)
            eng.wait_ge(v, c.n)

        def bc(x):
            return x[:, :, None].to_broadcast([P, self.z.NB, D])

        done(eng.tensor_reduce(self.mean[:, :], a, AX.X, ALU.add))
        done(eng.tensor_scalar(self.mean[:, :], self.mean[:, :], 1.0 / D, None, ALU.mult))
        done(eng.tensor_tensor(a, a, bc(self.mean), ALU.subtract))
        done(eng.tensor_tensor(self.d2[:, :, :], a, a, ALU.mult))
        done(eng.tensor_reduce(self.var[:, :], self.d2[:, :, :], AX.X, ALU.add))
        eng.tensor_scalar(self.var[:, :], self.var[:, :], 1.0 / D, LN_EPS, ALU.mult, ALU.add)\
           .then_inc(self.var_ready, 1)
        eng.wait_ge(self.root_ready, 1)
        done(eng.reciprocal(self.rs[:, :], self.rs[:, :]))
        newton_rsqrt(eng, v, c, self.var[:, :], self.rs[:, :], self.tt[:, :])
        done(eng.tensor_tensor(out, a, bc(self.rs), ALU.mult))


def node_stage(nc, z, m, sb, ps, sem, bias):
    NB = z.NB
    acc = m["acc"]
    with ExitStack() as ctx:
        rec = sb(ctx, "rec", [P, NB, H], fp32)
        bb = sb(ctx, "bb", [P, D], fp32)
        prod = sb(ctx, "prod", [P, NB, D], fp32)
        norm = Norm(z, ctx, sb, sem, "ln0")
        v, bias_in = sem(ctx, "v_node"), sem(ctx, "bias_in")
        block = ctx.enter_context(nc.Block())

        @block.sync
        def _(eng):
            eng.dma_start(bb[:, :], bias.rearrange("(o d) -> o d", o=1).to_broadcast([P, D])).then_inc(bias_in, 16)

        @block.scalar
        def _(eng):
            norm.scalar(eng)

        @block.vector
        def _(eng):
            c = Count()

            def done(ins):
                ins.then_inc(v, c.up() and 1)
                eng.wait_ge(v, c.n)

            done(eng.tensor_scalar(rec[:, :, :], acc[:, 0:NB, C:C + H], float(H), 1e-37, ALU.mult, ALU.max))
            done(eng.reciprocal(rec[:, :, :], rec[:, :, :]))
            eng.wait_ge(bias_in, 16)
            x = m["xn"][:, :, :]
            done(eng.tensor_tensor(x, x, bb[:, None, :].to_broadcast([P, NB, D]), ALU.add))
            for h in range(H):
                done(eng.tensor_tensor(prod[:, :, :], acc[:, 0:NB, h * D:(h + 1) * D],
                                       rec[:, :, h, None].to_broadcast([P, NB, D]), ALU.mult))
                done(eng.tensor_tensor(x, x, prod[:, :, :], ALU.add))
            norm.vector(eng, x, x, v, c)


def transform_stage(nc, z, m, sb, ps, sem, n, w):
    NB = z.NB
    with ExitStack() as ctx:
        wsb = sb(ctx, f"w{n}sb", [D, D], fp32)
        wrote = sem(ctx, f"wrote{n}")
        source = m["xn"] if n == 0 else m["hn"]
        gs = m["gs"]

        def finish(eng, i, psW, finished):
            g = gs[:, bass.ds(i * BC, BC), :]
            eng.tensor_tensor(g, psW[0][:, 0:BC * D].rearrange("p (b d) -> p b d", d=D),
                              m["dinv"][:, bass.ds(i * BC, BC)][:, :, None].to_broadcast([P, BC, D]),
                              ALU.mult).then_inc(finished, 1)

        def w_dma(eng, w_in):
            eng.dma_start(wsb[:, :], w).then_inc(w_in, 16)

        def tail(eng, finished, n_it):
            eng.wait_ge(finished, n_it)
            eng.dma_start(m["gtab"][n].rearrange("(b p) d -> p b d", p=P), gs[:, :, :]).then_inc(wrote, 16)
            eng.wait_ge(wrote, 16)

        if n == 0:
            degree_stage(nc, z, m, sb, ps, sem)
        chunk_transform(nc, z, ctx, sb, ps, sem, m, f"tr{n}", source, wsb[:, :], w_dma, D, finish, tail)


def degree_stage(nc, z, m, sb, ps, sem):
    with ExitStack() as ctx:
        tt = sb(ctx, "dtt", [P, z.NB], fp32)
        v, ready, root = sem(ctx, "v_deg"), sem(ctx, "deg_plus"), sem(ctx, "deg_root")
        block = ctx.enter_context(nc.Block())

        @block.scalar
        def _(eng):
            eng.wait_ge(ready, 1)
            eng.activation(m["dinv"][:, :], m["deg"][:, :], ACT.Sqrt).then_inc(root, 1)

        @block.vector
        def _(eng):
            c = Count()
            eng.tensor_scalar(m["deg"][:, :], m["deg"][:, :], 1.0, None, ALU.add).then_inc(ready, 1)
            eng.wait_ge(root, 1)
            eng.reciprocal(m["dinv"][:, :], m["dinv"][:, :]).then_inc(v, c.up() and 1)
            eng.wait_ge(v, c.n)
            newton_rsqrt(eng, v, c, m["deg"][:, :], m["dinv"][:, :], tt[:, :])


def gather_stage(nc, z, m, sb, ps, sem, n):
    n_it = z.NU // BU
    with ExitStack() as ctx:
        rd = sb(ctx, f"rd{n}", [P, z.TT, 2], fp32)
        idx = [sb(ctx, f"gidx{n}{q}", [P, BU * UT], i32) for q in range(2)]
        g = [sb(ctx, f"gx{n}{q}", [P, UT, D], fp32) for q in range(2 * BU)]
        one = [sb(ctx, f"oneg{n}{q}", [P, UT, P], fp32) for q in range(2)]
        psg = [ps(ctx, f"psg{n}{q}", [P, 512], fp32) for q in range(BU)]
        NS = 2 * BU
        rd_in, cleared, begun = sem(ctx, f"rd_in{n}"), sem(ctx, f"agg_zero{n}"), sem(ctx, f"begun{n}")
        idx_ready = [sem(ctx, f"gidx_ready{n}{q}") for q in range(2)]
        got, one_ready, summed, added = ([sem(ctx, f"{s}{n}_{j}") for j in range(NS)] for s in (
            "g_got", "g_one", "g_summed", "g_added"))
        block = ctx.enter_context(nc.Block())
        assert n_it % 2 == 1

        def bodies(eng, emit):
            with eng.Fori(0, n_it // 2) as i:
                for a in range(2):
                    emit(i, a)
            emit(n_it // 2, 0)

        @block.sync
        def _(eng):
            eng.dma_start(rd[:, :, :], m["rows_d"].rearrange("(p t) c -> p t c", p=P)).then_inc(rd_in, 16)

        @block.scalar
        def _(eng):
            eng.wait_ge(rd_in, 16)

            def emit(i, a):
                for j in range(BU):
                    eng.wait_ge(got[a * BU + j], i * 16 * UT)
                t = (2 * i + a) * BU * UT
                eng.copy(idx[a][:, :], rd[:, bass.ds(t, BU * UT) if not isinstance(i, int) else
                                          slice(t, t + BU * UT), 0].bitcast(i32)).then_inc(idx_ready[a], 1)

            bodies(eng, emit)

        @block.gpsimd
        def _(eng):
            eng.memset(m["agg"][:, :, :], 0.0).then_inc(cleared, 1)

            def emit(i, a):
                eng.wait_ge(idx_ready[a], i + 1)
                for j in range(BU):
                    s = a * BU + j
                    eng.wait_ge(summed[s], i)
                    eng.sem_inc(begun, 1)
                    for k in range(UT):
                        eng.indirect_dma_start(
                            out=g[s][:, k, :], out_offset=None, in_=m["gtab"][n],
                            in_offset=bass.IndirectOffsetOnAxis(ap=idx[a][:, j * UT + k:j * UT + k + 1], axis=0))\
                           .then_inc(got[s], 16)

            bodies(eng, emit)

        @block.vector
        def _(eng):
            eng.wait_ge(cleared, 1)
            eng.wait_ge(rd_in, 16)

            def places(i, a, j):
                s, q = a * BU + j, j % 2
                o, c = (s - 2, i + 1) if s >= 2 else (s - 2 + NS, i)
                eng.wait_ge(summed[o], c)
                for k in range(UT):
                    t = ((2 * i + a) * BU + j) * UT + k
                    eng.tensor_scalar(one[q][:, k, :], m["io128"][:, :],
                                      rd[:, bass.ds(t, 1) if not isinstance(i, int) else slice(t, t + 1), 1],
                                      None, ALU.is_equal).then_inc(one_ready[s], 1)

            def add(i, a, j):
                s = a * BU + j
                u = (2 * i + a) * BU + j
                row = m["blkS"][0:1, 1, bass.ds(u, 1) if not isinstance(i, int) else slice(u, u + 1)]
                b = eng.value_load(row, min_val=0, max_val=z.HB - 1)
                eng.wait_ge(summed[s], i + 1)
                o, c = (s - 1, i + 1) if s >= 1 else (NS - 1, i)
                eng.wait_ge(added[o], c)
                t = m["agg"][:, bass.ds(b, 1), :].rearrange("p o c -> p (o c)")
                eng.tensor_tensor(t, t, psg[j][:, 0:D], ALU.add).then_inc(added[s], 1)

            def emit(i, a):
                for j in range(BU):
                    places(i, a, j)
                    add(i, a, j)

            bodies(eng, emit)

        @block.tensor
        def _(eng):
            def emit(i, a):
                for j in range(BU):
                    s, q = a * BU + j, j % 2
                    o, c = (s - BU, i + 1) if a else (s + BU, i)
                    eng.wait_ge(one_ready[s], (i + 1) * UT)
                    eng.wait_ge(got[s], (i + 1) * 16 * UT)
                    eng.wait_ge(added[o], c)
                    for k in range(UT):
                        mm = eng.matmul(psg[j][:, 0:D], one[q][:, k, :], g[s][:, k, :], start=(k == 0),
                                        stop=(k == UT - 1))
                    mm.then_inc(summed[s], 1)

            bodies(eng, emit)


def close_stage(nc, z, m, sb, ps, sem, n, b, out):
    NB = z.NB
    with ExitStack() as ctx:
        bb = sb(ctx, f"cb{n}", [P, D], fp32)
        v, b_in = sem(ctx, f"v_close{n}"), sem(ctx, f"cb_in{n}")
        norm = Norm(z, ctx, sb, sem, "ln1") if n else None
        normed = sem(ctx, f"normed{n}")
        out_done = sem(ctx, f"out_done{n}")
        block = ctx.enter_context(nc.Block())
        hn, x = m["hn"][:, :, :], m["xn"][:, :, :]

        @block.sync
        def _(eng):
            eng.dma_start(bb[:, :], b.rearrange("(o d) -> o d", o=1).to_broadcast([P, D])).then_inc(b_in, 16)
            if n:
                eng.wait_ge(normed, 1)
                whole = z.N // P
                eng.dma_start(out[0:whole * P, :].rearrange("(b p) d -> p b d", p=P), m["hn"][:, 0:whole, :])\
                   .then_inc(out_done, 16)
                if z.N % P:
                    eng.dma_start(out[whole * P:z.N, :], m["hn"][0:z.N % P, whole, :]).then_inc(out_done, 16)
                eng.wait_ge(out_done, 32 if z.N % P else 16)

        @block.scalar
        def _(eng):
            if n:
                norm.scalar(eng)

        @block.vector
        def _(eng):
            c = Count()

            def done(ins):
                ins.then_inc(v, c.up() and 1)
                eng.wait_ge(v, c.n)

            eng.wait_ge(b_in, 16)
            done(eng.tensor_tensor(hn, m["agg"][:, 0:NB, :], m["gs"][:, :, :], ALU.add))
            done(eng.tensor_tensor(hn, hn, m["dinv"][:, :, None].to_broadcast([P, NB, D]), ALU.mult))
            done(eng.tensor_tensor(hn, hn, bb[:, None, :].to_broadcast([P, NB, D]), ALU.add))
            if n:
                done(eng.scalar_tensor_tensor(x, hn, 0.0, x, ALU.max, ALU.add))
                norm.vector(eng, x, hn, v, c)
                eng.sem_inc(normed, 1)


_INS = ['x', 'src', 'dst', 'edge_attr_64', 'L0_gnn_W', 'L0_gnn_att', 'L0_gnn_bias', 'L0_gnn_bn_gamma',
        'L0_gnn_bn_beta', 'L1_gnn_W1', 'L1_gnn_b1', 'L1_gnn_W2', 'L1_gnn_b2']


def kernel(**inputs):
    import numpy as _np
    import concourse.bacc as _bacc
    from concourse import mybir as _mybir
    from concourse.bass_utils import run_bass_kernel_spmd as _run

    nc = _bacc.Bacc("TRN2", target_bir_lowering=False, num_devices=1)
    arrays, args = {}, []
    for name in _INS:
        a = _np.ascontiguousarray(inputs[name])
        arrays[f"in_{name}_dram"] = a
        args.append(nc.dram_tensor(f"in_{name}_dram", a.shape, _mybir.dt.from_np(a.dtype), kind="ExternalInput").ap())
    shape = inputs['x'].shape
    args.append(nc.dram_tensor("out_0_dram", shape, _mybir.dt.float32, kind="ExternalOutput").ap())
    gnn_kernel(nc, *args)
    r = _run(nc, [arrays], core_ids=[0])
    return r.results[0]["out_0_dram"]
```

```python
import concourse.bass as bass
from concourse import mybir
from contextlib import ExitStack

fp32 = mybir.dt.float32
bf16 = mybir.dt.bfloat16
i32 = mybir.dt.int32
ALU = mybir.AluOpType
ACT = mybir.ActivationFunctionType
AX = mybir.AxisListType

P = 128
D = 64
H = 4
C = H * D
K = 8
UT = 2
BU = 6
PRE = 3
BC = 7
GD = 16
GB = P // GD
GT = 5
CODE = 1024
EXACT = 256
RANGE = 60.0
fp16 = mybir.dt.float16
CAP_SP = 20.0
BN_EPS = 1e-5
LN_EPS = 1e-5


class Sizes:

    def __init__(self, nodes, edges):
        self.N, self.E = nodes, edges
        self.NB = -(-nodes // (P * BC)) * BC
        self.HB = self.NB + 1
        self.NG = 2 * -(-edges // (2 * P * K))
        self.rem = edges - (self.NG - 1) * P * K
        assert self.rem > 0 and self.rem < P * K and self.rem % K
        units = (self.NG * P * K + self.HB * (P * UT - 1)) // (P * UT)
        self.NU = (-(-units // BU) | 1) * BU
        self.TT = self.NU * UT
        self.UC = max(2, -(-self.NU // P))
        self.GC = self.NB * GD
        self.NR = self.NB * GB
        assert self.GC < CODE and self.GC <= 1024


class Count:

    def __init__(self):
        self.n = 0

    def up(self):
        self.n += 1
        return self.n


def span(a, w):
    return slice(a, a + w) if isinstance(a, int) else bass.ds(a, w)


def wait(eng, semaphore, value):
    if not isinstance(value, int) or value > 0:
        eng.wait_ge(semaphore, value)


def rounds(eng, n, emit, start=0):
    if n - start > 0:
        emit(start)
    if n - start > 2:
        with eng.Fori(start + 1, n - 1) as i:
            emit(i)
    if n - start > 1:
        emit(n - 1)


def paired_rounds(eng, n, emit):
    def two(i):
        emit(2 * i)
        emit(2 * i + 1)

    rounds(eng, n // 2, two)
    emit(n - 1)


def before(i, j, depth, width):
    return (j - depth, i + 1) if j >= depth else (j - depth + width, i)


def seg(i, j, depth):
    return (i + 1, j - depth) if j >= depth else (i, j)


def distances(eng, dist, iota, minus):
    for k in range(dist.shape[1]):
        ins = eng.activation(dist[:, k, :], iota, ACT.Abs, bias=minus(k))
    return ins


def near(eng, out, dist):
    return eng.activation(out, dist[:, :, :], ACT.Relu, bias=1.0, scale=-1.0)


def gnn_kernel(nc, x, src, dst, ea, W, att, bias, gamma, beta, W1, b1, W2, b2, out):
    z = Sizes(x.shape[0], src.shape[0])
    NB, HB = z.NB, z.HB
    top = ExitStack()
    stages = {}

    def sb(ctx, name, shape, dt):
        return ctx.enter_context(nc.sbuf_tensor(name, shape, dt))

    def ps(ctx, name, shape, dt):
        return ctx.enter_context(nc.psum_tensor(name, shape, dt))

    def sem(ctx, name):
        if ctx not in stages:
            stages[ctx] = []
            ctx.callback(give_back, ctx)
        stages[ctx].append(nc.alloc_semaphore(name))
        return stages[ctx][-1]

    def give_back(ctx):
        nc.clear_and_free_semaphores(stages.pop(ctx))
        nc.all_engine_barrier()

    with top:
        m = {"x_in": x}
        m["rows"] = nc.dram_tensor("rows", (P * z.TT, D + 2), fp32).ap()
        m["rows_d"] = nc.dram_tensor("rows_d", (P * z.TT, 2), fp32).ap()
        m["outj"] = nc.dram_tensor("outj", (P, z.TT * C), fp32).ap()
        m["blk"] = nc.dram_tensor("blk", (2, P * z.UC), i32).ap()
        m["pairs"] = nc.dram_tensor("pairs", (z.NG * P * K + GT * P, 2), fp32).ap()
        m["start"] = nc.dram_tensor("start", (1, z.NR), i32).ap()
        m["adj"] = nc.dram_tensor("adj", (NB, P, NB * P), bf16).ap()
        m["gtab"] = [nc.dram_tensor(f"gtab{n}", (NB * P, D), fp32).ap() for n in range(2)]
        m["io50"] = sb(top, "io50", [P, HB], bf16)
        m["io128"] = sb(top, "io128", [P, P], fp32)
        m["io128b"] = sb(top, "io128b", [P, P], bf16)
        m["io784"] = sb(top, "io784", [P, z.GC], fp16)
        m["codes"] = sb(top, "codes", [P, z.NR], fp32)
        m["pidx"] = sb(top, "pidx", [P, 1], fp32)
        m["ident"] = sb(top, "ident", [P, P], fp32)
        m["identb"] = sb(top, "identb", [P, P], bf16)
        m["tri"] = sb(top, "tri", [P, P], bf16)
        m["onesb"] = sb(top, "onesb", [P, P], bf16)
        m["onesf"] = sb(top, "onesf", [P, P], fp32)
        m["startS"] = sb(top, "startS", [1, z.NR], i32)
        m["blkS"] = sb(top, "blkS", [1, 2, P * z.UC], i32)
        m["base"] = sb(top, "base", [P, 2, HB], fp32)
        m["deg"] = sb(top, "deg", [P, NB], fp32)
        m["dinv"] = sb(top, "dinv", [P, NB], fp32)
        m["bad"] = sb(top, "bad", [P, 1], fp32)
        m["flag"] = sb(top, "flag", [1, 2], i32)
        m["xn"] = sb(top, "xn", [P, NB, D], fp32)
        m["hib"] = sb(top, "hib", [P, 2, z.NG * K], bf16)
        m["nlo"] = sb(top, "nlo", [P, z.NG * K], fp32)
        m["lo"] = sb(top, "lo", [P, z.NG * K], fp32)
        m["val"] = sb(top, "val", [P, 2, z.NG * K], i32)
        key_stage(nc, z, m, sb, ps, sem, x, src, dst)
        sort_stage(nc, z, m, sb, ps, sem, 0, ea)
        degree_stage(nc, z, m, sb, ps, sem)
        with ExitStack() as edge:
            m["nloA"] = sb(edge, "nloA", [P, z.TT], fp32)
            m["alpha"] = sb(edge, "alpha", [P, z.TT, H], fp32)
            m["top"] = sb(edge, "top", [P, H], fp32)
            with ExitStack() as ptab:
                m["P3"] = [sb(ptab, f"P3_{n}", [P, HB * C], bf16) for n in range(3)]
                m["Wsb"] = sb(ptab, "Wsb", [P, C], fp32)
                table_stage(nc, z, m, sb, ps, sem, W)
                edge_stage(nc, z, m, sb, ps, sem, att)
            softmax_stage(nc, z, m, sb, ps, sem, gamma, beta)
            with nc.If(nc.values_load(m["flag"][0:1, 1:2], min_val=0, max_val=1)):
                node_max_stage(nc, z, m, sb, ps, sem)
            weight_stage(nc, z, m, sb, ps, sem)
            m["acc"] = sb(edge, "acc", [P, HB, C + H], fp32)
            message_stage(nc, z, m, sb, ps, sem)
            node_stage(nc, z, m, sb, ps, sem, bias)
        with ExitStack() as conv:
            m["hn"] = sb(conv, "hn", [P, NB, D], fp32)
            m["gs"] = sb(conv, "gs", [P, NB, D], fp32)
            m["agg"] = sb(conv, "agg", [P, HB, D], fp32)
            for n, (w, b) in enumerate(((W1, b1), (W2, b2))):
                transform_stage(nc, z, m, sb, ps, sem, n, w)
                with nc.If(nc.values_load(m["flag"][0:1, 0:1], min_val=0, max_val=1)):
                    if n == 0:
                        sort_stage(nc, z, m, sb, ps, sem, 1)
                    gather_stage(nc, z, m, sb, ps, sem, n)
                with nc.Else():
                    dense_stage(nc, z, m, sb, ps, sem, n)
                close_stage(nc, z, m, sb, ps, sem, n, b, out)


def key_stage(nc, z, m, sb, ps, sem, x, src, dst):
    NB, HB, NG, T = z.NB, z.HB, z.NG, z.NG * K
    with ExitStack() as ctx:
        key = sb(ctx, "key", [P, 2, T], i32)
        tmp = sb(ctx, "keytmp", [P, 2, T], i32)
        neg = sb(ctx, "keyneg", [P, 2, T], fp32)
        zer = sb(ctx, "zer", [P, K * HB], bf16)
        oh = [sb(ctx, f"oh{j}", [P, 2, K * HB], bf16) for j in range(2)]
        cnt = sb(ctx, "cnt", [P, 2, HB], fp32)
        cnti = sb(ctx, "cnti", [P, 2, HB], i32)
        uni = sb(ctx, "uni", [P, 2, HB], fp32)
        incl = sb(ctx, "incl", [P, 2, HB], fp32)
        uidx = sb(ctx, "uidx", [P, z.UC], fp32)
        cmp = sb(ctx, "cmp", [P, 2, z.UC, HB], fp32)
        blkf = sb(ctx, "blkf", [P, 2, z.UC], fp32)
        blki = sb(ctx, "blki", [P, 2, z.UC], i32)
        fill = sb(ctx, "fill", [P, BU * UT, D + 2], fp32)
        nxt = sb(ctx, "nxt", [P, T], i32)
        qb = sb(ctx, "qb", [P, T], bf16)
        ohq = [sb(ctx, f"ohq{j}", [P, K, GB], bf16) for j in range(2)]
        cnt8 = sb(ctx, "cnt8", [GB, HB], fp32)
        tri8 = sb(ctx, "tri8", [GB, GB], fp32)
        first = sb(ctx, "first", [P, HB], fp32)
        st8 = sb(ctx, "st8", [GB, NB], i32)
        full8 = sb(ctx, "full8", [GB, 1], fp32)
        pair = sb(ctx, "pair", [P, T, 2], fp32)
        none = sb(ctx, "none", [P, GT, 2], fp32)
        psq = ps(ctx, "psq", [P, 512], fp32)
        psw = ps(ctx, "psw", [P, 512], fp32)
        psc = [ps(ctx, f"psc{n}", [P, 512], fp32) for n in range(2)]
        made = sem(ctx, "made")
        cleared = sem(ctx, "cleared")
        loaded = sem(ctx, "loaded")
        x_in = sem(ctx, "x_in")
        filled = sem(ctx, "filled")
        v = sem(ctx, "v_key")
        oh_ready = [sem(ctx, f"oh_ready{j}") for j in range(2)]
        oh_used = [sem(ctx, f"oh_used{j}") for j in range(2)]
        counted = sem(ctx, "counted")
        blk_ready = sem(ctx, "blk_ready")
        blk_out = sem(ctx, "blk_out")
        group_counts = sem(ctx, "group_counts")
        within = sem(ctx, "within")
        pairs_ready = sem(ctx, "pairs_ready")
        pairs_out = sem(ctx, "pairs_out")
        starts_ready = sem(ctx, "starts_ready")
        starts_out = sem(ctx, "starts_out")
        block = ctx.enter_context(nc.Block())
        body = (NG - 1) * P * K

        def load_keys(eng, to, a, base):
            full, tail = (z.rem - base) // K, (z.rem - base) % K
            eng.dma_start(to[:, 0:T - K].rearrange("p (g k) -> p g k", k=K),
                          a[base:base + body].rearrange("(g p k) -> p g k", p=P, k=K)).then_inc(loaded, 16)
            if full:
                eng.dma_start(to[0:full, T - K:T],
                              a[base + body:base + body + full * K].rearrange("(p k) -> p k", k=K))\
                   .then_inc(loaded, 16)
            if tail:
                eng.dma_start(to[full:full + 1, T - K:T - K + tail],
                              a[base + body + full * K:z.E].rearrange("(o k) -> o k", o=1)).then_inc(loaded, 16)

        loads = sum(1 + (r >= K) + (r % K > 0) for r in (z.rem, z.rem, z.rem - 1))

        @block.sync
        def _(eng):
            eng.wait_ge(cleared, 4)
            load_keys(eng, key[:, 0, :], src, 0)
            load_keys(eng, key[:, 1, :], dst, 0)
            load_keys(eng, nxt[:, :], dst, 1)
            whole = z.N // P
            eng.dma_start(m["xn"][:, 0:whole, :], x[0:whole * P, :].rearrange("(b p) d -> p b d", p=P))\
               .then_inc(x_in, 16)
            if z.N % P:
                eng.dma_start(m["xn"][0:z.N % P, whole, :], x[whole * P:z.N, :]).then_inc(x_in, 16)
            eng.wait_ge(blk_ready, 1)
            eng.dma_start(m["blk"].rearrange("n (p c) -> p n c", c=z.UC), blki[:, :, :]).then_inc(blk_out, 16)
            eng.wait_ge(blk_out, 16)
            eng.dma_start(m["blkS"][0:1, :, :], m["blk"].rearrange("(o n) c -> o n c", o=1)).then_inc(blk_out, 16)
            eng.wait_ge(starts_ready, 1)
            with nc.allow_non_contiguous_dma(reason="a few hundred numbers"):
                eng.dma_start(m["start"][0, :].rearrange("(b q) -> q b", q=GB), st8[:, :]).then_inc(starts_out, 16)
            eng.wait_ge(starts_out, 16)
            eng.dma_start(m["startS"][0:1, :], m["start"]).then_inc(starts_out, 16)
            eng.wait_ge(starts_out, 32)
            eng.wait_ge(blk_out, 32)
            eng.wait_ge(x_in, 32 if z.N % P else 16)

        @block.scalar
        def _(eng):
            eng.wait_ge(cleared, 6)
            rows = m["rows"].rearrange("(p t) c -> p t c", p=P)
            eng.dma_start(m["pairs"][NG * P * K:, :].rearrange("(p k) c -> p k c", k=GT), none[:, :, :])\
               .then_inc(filled, 16)
            for t in range(0, z.TT, BU * UT):
                eng.dma_start(rows[:, t:t + BU * UT, :], fill[:, :, :]).then_inc(filled, 16)
            eng.wait_ge(pairs_ready, 1)
            eng.dma_start(m["pairs"][0:NG * P * K, :].rearrange("(g p k) c -> p g (k c)", p=P, k=K),
                          pair[:, :, :].rearrange("p (g k) c -> p g (k c)", k=K)).then_inc(pairs_out, 16)
            eng.wait_ge(filled, 16 * (z.TT // (BU * UT) + 1))
            eng.wait_ge(pairs_out, 16)

        @block.gpsimd
        def _(eng):
            eng.memset(key[:, :, :], NB * P).then_inc(cleared, 1)
            eng.memset(nxt[:, :], NB * P).then_inc(cleared, 1)
            eng.memset(m["xn"][:, :, :], 0.0).then_inc(cleared, 1)
            eng.memset(zer[:, :], 0.0).then_inc(cleared, 1)
            eng.memset(none[:, :, :], -1.0).then_inc(cleared, 1)
            eng.memset(fill[:, :, :], 0.0).then_inc(made, 1)
            eng.wait_ge(made, 1)
            eng.memset(fill[:, :, D:D + 1], 1.0).then_inc(cleared, 1)
            eng.iota(m["io50"][:, :], [[1, HB]], base=0, channel_multiplier=0,
                     allow_small_or_imprecise_dtypes=True).then_inc(made, 1)
            eng.iota(m["io128"][:, :], [[1, P]], base=0, channel_multiplier=0,
                     allow_small_or_imprecise_dtypes=True).then_inc(made, 1)
            eng.iota(m["io128b"][:, :], [[1, P]], base=0, channel_multiplier=0,
                     allow_small_or_imprecise_dtypes=True).then_inc(made, 1)
            eng.iota(m["pidx"][:, :], [[1, 1]], base=0, channel_multiplier=1,
                     allow_small_or_imprecise_dtypes=True).then_inc(made, 1)
            eng.iota(uidx[:, :], [[1, z.UC]], base=0, channel_multiplier=z.UC,
                     allow_small_or_imprecise_dtypes=True).then_inc(made, 1)
            eng.iota(m["io784"][:, :], [[1, z.GC]], base=0, channel_multiplier=0,
                     allow_small_or_imprecise_dtypes=True).then_inc(made, 1)
            eng.iota(m["codes"][:, :], [[CODE, z.NR]], base=0, channel_multiplier=0,
                     allow_small_or_imprecise_dtypes=True).then_inc(made, 1)
            eng.memset(m["onesb"][:, :], 1.0).then_inc(made, 1)
            eng.memset(m["onesf"][:, :], 1.0).then_inc(made, 1)

        @block.vector
        def _(eng):
            eng.wait_ge(made, 10)
            c = Count()
            eng.tensor_scalar(tri8[:, :], m["io128"][0:GB, 0:GB], m["pidx"][0:GB, 0:1], None,
                              ALU.is_gt).then_inc(v, c.up() and 1)
            eng.tensor_scalar(m["ident"][:, :], m["io128"][:, :], m["pidx"][:, 0:1], None,
                              ALU.is_equal).then_inc(v, c.up() and 1)
            eng.tensor_scalar(m["identb"][:, :], m["io128"][:, :], m["pidx"][:, 0:1], None,
                              ALU.is_equal).then_inc(v, c.up() and 1)
            eng.tensor_scalar(m["tri"][:, :], m["io128"][:, :], m["pidx"][:, 0:1], None,
                              ALU.is_gt).then_inc(v, c.up() and 1)
            eng.wait_ge(loaded, 16 * loads)
            eng.tensor_scalar(tmp[:, :, :], key[:, :, :], 7, None, ALU.arith_shift_right).then_inc(v, c.up() and 1)
            eng.wait_ge(v, c.n)
            eng.tensor_copy(m["hib"][:, :, :], tmp[:, :, :]).then_inc(v, c.up() and 1)
            eng.wait_ge(v, c.n)
            eng.tensor_scalar(tmp[:, :, :], key[:, :, :], P - 1, None, ALU.bitwise_and).then_inc(v, c.up() and 1)
            eng.tensor_scalar(neg[:, :, :], key[:, :, :], float(NB * P), float(-P), ALU.is_ge,
                              ALU.mult).then_inc(v, c.up() and 1)
            for n in range(2):
                eng.tensor_scalar(m["val"][:, 1 - n, :], key[:, n, :], float(z.N - 1), None,
                                  ALU.min).then_inc(v, c.up() and 1)
            eng.wait_ge(v, c.n)
            eng.tensor_tensor(m["lo"][:, :], tmp[:, 1, :], neg[:, 1, :], ALU.add).then_inc(v, c.up() and 1)
            eng.scalar_tensor_tensor(m["nlo"][:, :], tmp[:, 0, :], -1.0, neg[:, 0, :], ALU.mult,
                                     ALU.subtract).then_inc(v, c.up() and 1)
            eng.wait_ge(v, c.n)
            eng.tensor_copy(pair[:, :, 0], m["nlo"][:, :]).then_inc(v, c.up() and 1)
            eng.tensor_scalar(tmp[:, 0, :], key[:, 1, :], 4, None, ALU.arith_shift_right).then_inc(v, c.up() and 1)
            eng.tensor_scalar(tmp[:, 1, :], key[:, 1, :], GD - 1, None, ALU.bitwise_and).then_inc(v, c.up() and 1)
            eng.tensor_scalar(neg[:, 0, :], m["hib"][:, 0, :], float(GD), None, ALU.mult).then_inc(v, c.up() and 1)
            eng.wait_ge(v, c.n)
            eng.scalar_tensor_tensor(neg[:, 1, :], tmp[:, 0, :], float(CODE), tmp[:, 1, :], ALU.mult,
                                     ALU.add).then_inc(v, c.up() and 1)
            eng.wait_ge(v, c.n)
            eng.tensor_tensor(pair[:, :, 1], neg[:, 0, :], neg[:, 1, :], ALU.add).then_inc(v, c.up() and 1)
            eng.tensor_scalar(tmp[:, 1, :], tmp[:, 0, :], GB - 1, None, ALU.bitwise_and).then_inc(v, c.up() and 1)
            eng.wait_ge(v, c.n)
            eng.tensor_tensor(neg[:, 0, :], key[:, 1, :], nxt[:, :], ALU.is_gt).then_inc(v, c.up() and 1)
            eng.wait_ge(v, c.n)
            eng.tensor_copy(qb[:, :], tmp[:, 1, :]).then_inc(pairs_ready, 1)
            eng.tensor_reduce(m["bad"][:, :], neg[:, 0, :], AX.X, ALU.add).then_inc(v, c.up() and 1)
            eng.wait_ge(v, c.n)
            eng.wait_ge(pairs_ready, 1)

            def one_hots(i):
                for j in range(2):
                    g = span((2 * i + j) * K, K)
                    wait(eng, oh_used[j], i)
                    for n in range(2):
                        eng.tensor_tensor(
                            oh[j][:, n, :].rearrange("p (k h) -> p k h", h=HB),
                            m["io50"][:, None, :].to_broadcast([P, K, HB]),
                            m["hib"][:, n, g][:, :, None].to_broadcast([P, K, HB]),
                            ALU.is_equal).then_inc(oh_ready[j], 1)
                    eng.tensor_tensor(ohq[j][:, :, :], m["io50"][:, None, 0:GB].to_broadcast([P, K, GB]),
                                      qb[:, g][:, :, None].to_broadcast([P, K, GB]),
                                      ALU.is_equal).then_inc(oh_ready[j], 1)

            rounds(eng, NG // 2, one_hots)
            eng.wait_ge(counted, 1)
            for n in range(2):
                eng.tensor_reduce(cnt[:, n, :], psc[n][:, 0:K * HB].rearrange("p (k h) -> p h k", h=HB),
                                  AX.X, ALU.add).then_inc(v, c.up() and 1)
            eng.tensor_copy(cnt8[:, :], psq[0:GB, 0:HB]).then_inc(group_counts, 1)
            eng.wait_ge(v, c.n)
            eng.tensor_tensor_scan(first[:, :], m["onesf"][:, 0:HB], cnt[:, 1, :], 0.0, ALU.mult,
                                   ALU.add).then_inc(v, c.up() and 1)
            eng.wait_ge(group_counts, 1)
            eng.tensor_reduce(full8[:, :], cnt8[:, 0:NB], AX.X, ALU.max).then_inc(v, c.up() and 1)
            eng.wait_ge(v, c.n)
            eng.tensor_scalar(full8[:, :], full8[:, :], float(GT * P), None, ALU.is_gt).then_inc(v, c.up() and 1)
            eng.tensor_tensor(first[:, :], first[:, :], cnt[:, 1, :], ALU.subtract).then_inc(v, c.up() and 1)
            eng.wait_ge(v, c.n)
            eng.tensor_tensor(m["bad"][0:GB, :], m["bad"][0:GB, :], full8[:, :], ALU.add).then_inc(v, c.up() and 1)
            eng.wait_ge(within, 1)
            eng.tensor_tensor(st8[:, :], psw[0:GB, 0:NB], first[0:GB, 0:NB], ALU.add).then_inc(starts_ready, 1)
            eng.tensor_scalar(cnti[:, :, :], cnt[:, :, :], float(P * UT - 1), None, ALU.add).then_inc(v, c.up() and 1)
            eng.wait_ge(v, c.n)
            eng.tensor_scalar(cnti[:, :, :], cnti[:, :, :], 8, None, ALU.arith_shift_right).then_inc(v, c.up() and 1)
            eng.wait_ge(v, c.n)
            eng.tensor_copy(uni[:, :, :], cnti[:, :, :]).then_inc(v, c.up() and 1)
            eng.wait_ge(v, c.n)
            for n in range(2):
                eng.tensor_tensor_scan(incl[:, n, :], m["onesf"][:, 0:HB], uni[:, n, :], 0.0, ALU.mult,
                                       ALU.add).then_inc(v, c.up() and 1)
            eng.wait_ge(v, c.n)
            eng.tensor_tensor(cnt[:, :, :], incl[:, :, :], uni[:, :, :], ALU.subtract).then_inc(v, c.up() and 1)
            eng.wait_ge(v, c.n)
            eng.tensor_scalar(m["base"][:, :, :], cnt[:, :, :], float(P * UT), None, ALU.mult).then_inc(v, c.up() and 1)
            for n in range(2):
                eng.tensor_tensor(cmp[:, n, :, :], uidx[:, :, None].to_broadcast([P, z.UC, HB]),
                                  incl[:, n, None, :].to_broadcast([P, z.UC, HB]), ALU.is_ge).then_inc(v, c.up() and 1)
            eng.wait_ge(v, c.n)
            for n in range(2):
                eng.tensor_reduce(blkf[:, n, :], cmp[:, n, :, :], AX.X, ALU.add).then_inc(v, c.up() and 1)
            eng.wait_ge(v, c.n)
            eng.tensor_scalar(blki[:, :, :], blkf[:, :, :], float(NB), None, ALU.min).then_inc(blk_ready, 1)

        @block.tensor
        def _(eng):
            eng.wait_ge(cleared, 4)
            eng.wait_ge(made, 10)
            for n in range(2):
                eng.matmul(psc[n][:, 0:K * HB], m["onesb"][:, :], zer[:, :], start=True, stop=False,
                           skip_group_check=True)
            eng.matmul(psq[0:GB, 0:HB], zer[:, 0:GB], zer[:, 0:HB], start=True, stop=False, skip_group_check=True)

            def counts(i):
                for j in range(2):
                    eng.wait_ge(oh_ready[j], i * 3 + 3)
                    for n in range(2):
                        eng.matmul(psc[n][:, 0:K * HB], m["onesb"][:, :], oh[j][:, n, :], start=False,
                                   stop=False, skip_group_check=True)
                    for k in range(K):
                        mm = eng.matmul(psq[0:GB, 0:HB], ohq[j][:, k, :], oh[j][:, 1, k * HB:(k + 1) * HB],
                                        start=False, stop=False, skip_group_check=True)
                    mm.then_inc(oh_used[j], 1)

            rounds(eng, NG // 2, counts)
            for n in range(2):
                eng.matmul(psc[n][:, 0:K * HB], m["onesb"][:, :], zer[:, :], start=False, stop=True,
                           skip_group_check=True)
            eng.matmul(psq[0:GB, 0:HB], zer[:, 0:GB], zer[:, 0:HB], start=False, stop=True,
                       skip_group_check=True).then_inc(counted, 1)
            eng.wait_ge(group_counts, 1)
            eng.matmul(psw[0:GB, 0:NB], tri8[:, :], cnt8[:, 0:NB], start=True, stop=True).then_inc(within, 1)


def sort_stage(nc, z, m, sb, ps, sem, n, ea=None):
    NB, HB, NG, T = z.NB, z.HB, z.NG, z.NG * K
    by_src = n == 0
    W = D + 2 if by_src else 2
    table = m["rows"] if by_src else m["rows_d"]
    n_sort, n_adj = NG // 2, NB
    n_both = min(n_adj, (n_sort - 1) // 2) if by_src else 0
    with ExitStack() as ctx:
        rows = [sb(ctx, f"rowS{n}{j}", [P, K, W], fp32) for j in range(2)]
        oh = [sb(ctx, f"ohr{n}{j}", [P, 1 + by_src, K + 1, HB], bf16) for j in range(2)]
        ranks = sb(ctx, f"ranks{n}", [P, K, HB], fp32)
        posf = sb(ctx, f"posf{n}", [P, K], fp32)
        posi = sb(ctx, f"posi{n}", [P, K], i32)
        lane = sb(ctx, f"lane{n}", [P, K], i32)
        tile = sb(ctx, f"tile{n}", [P, K], i32)
        idx = [sb(ctx, f"idx{n}{j}", [P, K], i32) for j in range(2)]
        psr = [ps(ctx, f"psr{n}{j}", [P, 512], fp32) for j in range(2)]
        cleared = sem(ctx, f"ohpad{n}_")
        ea_in = [sem(ctx, f"ea_in{n}_{j}") for j in range(2)]
        sent = [sem(ctx, f"sent{n}_{j}") for j in range(2)]
        oh_ready = [sem(ctx, f"ohr_ready{n}_{j}") for j in range(2)]
        oh_used = [sem(ctx, f"ohr_used{n}_{j}") for j in range(2)]
        ranked = [sem(ctx, f"ranked{n}_{j}") for j in range(2)]
        summed = [sem(ctx, f"summed{n}_{j}") for j in range(2)]
        idx_ready = [sem(ctx, f"idx_ready{n}_{j}") for j in range(2)]
        v = sem(ctx, f"v_sort{n}")
        begun = sem(ctx, f"scatter_begun{n}")
        if by_src:
            lob = sb(ctx, "lob", [P, T], bf16)
            ohlo = [sb(ctx, f"ohlo{j}", [P, K, P], bf16) for j in range(2)]
            psd = ps(ctx, "psd", [P, 512], fp32)
            deg_ready, lob_ready = sem(ctx, "deg_ready"), sem(ctx, "lob_ready")
            pair = [sb(ctx, f"pair{a}", [P, GT, 2], fp32) for a in range(GB)]
            code = [sb(ctx, f"code{r}", [P, GT], fp32) for r in range(2)]
            one_s = [sb(ctx, f"one_s{r}", [P, GT, P], bf16) for r in range(2)]
            one_c = [sb(ctx, f"one_c{r}", [P, GT, z.GC], bf16) for r in range(2)]
            cnts = [sb(ctx, f"cnts{u}", [P, NB, GB, GD], bf16) for u in range(2)]
            psa = [ps(ctx, f"psa{r}", [P, 2, 512], fp32) for r in range(2)]
            halves = ((0, -(-NB // 2)), (-(-NB // 2), NB // 2))
            dist = [sb(ctx, f"dist{r}", [P, GT, P], bf16) for r in range(2)]
            pair_in, code_ready, cols_ready, places_ready, built, copied = (
                [sem(ctx, f"a_{s}{a}") for a in range(GB)] for s in
                ("pair_in", "code", "cols", "places", "built", "copied"))
            dist_ready = sem(ctx, "a_dist")
            stored = [sem(ctx, f"adj_stored{u}") for u in range(2)]
        else:
            filld = sb(ctx, "filld", [P, z.TT, 2], fp32)
            filled, fill_ready = sem(ctx, "filled_d"), sem(ctx, "filld_ready")
        block = ctx.enter_context(nc.Block())
        full, tail = z.rem // K, z.rem % K
        if by_src:
            ea_g = ea[0:(NG - 1) * P * K, :].rearrange("(g p k) d -> g p k d", p=P, k=K)
            last = ea[(NG - 1) * P * K:z.E, :]

        @block.sync
        def _(eng):
            def load(i, j):
                wait(eng, sent[j], i * 16 * K)
                if isinstance(i, int) and 2 * i + j == NG - 1:
                    if full:
                        eng.dma_start(rows[j][0:full, :, 0:D], last[0:full * K, :].rearrange("(p k) d -> p k d", k=K))\
                           .then_inc(ea_in[j], 16)
                    eng.dma_start(rows[j][full:full + 1, 0:tail, 0:D],
                                  last[full * K:, :].rearrange("(p k) d -> p k d", p=1)).then_inc(ea_in[j], 16)
                else:
                    g = 2 * i + j
                    a = ea_g[g] if isinstance(g, int) else ea_g[bass.ds(g, 1)].rearrange("o p k d -> (o p) k d")
                    eng.dma_start(rows[j][:, :, 0:D], a).then_inc(ea_in[j], 16)

            def load_pairs(i, a):
                e = eng.value_load(m["startS"][0:1, span(i * GB + a, 1)], min_val=0, max_val=NG * P * K)
                if not isinstance(i, int) or i > 0:
                    eng.wait_ge(dist_ready, (i - 1) * GB + a + 1)
                wait(eng, code_ready[a], i)
                eng.dma_start(pair[a][:, :, :].rearrange("p k c -> p (k c)"),
                              m["pairs"][bass.ds(e, GT * P), :].rearrange("(p k) c -> p (k c)", k=GT))\
                   .then_inc(pair_in[a], 16)

            if by_src:
                def pairs_ahead(b, a):
                    if not (isinstance(b, int) and b == n_adj - 1 and a + GB // 2 >= GB):
                        load_pairs(*seg(b, a + GB // 2, GB))

                def together(b):
                    for s in range(4):
                        load(b * 2 + s // 2, s % 2)
                        pairs_ahead(b, 2 * s)
                        pairs_ahead(b, 2 * s + 1)

                def alone(i):
                    for j in range(2):
                        load(i, j)

                def rest(b):
                    for a in range(GB):
                        pairs_ahead(b, a)

                for a in range(GB // 2):
                    load_pairs(0, a)
                rounds(eng, n_both, together)
                rounds(eng, n_sort, alone, 2 * n_both)
                rounds(eng, n_adj, rest, n_both)
            else:
                eng.wait_ge(fill_ready, 2)
                eng.dma_start(m["rows_d"].rearrange("(p t) c -> p t c", p=P), filld[:, :, :]).then_inc(filled, 16)

        @block.gpsimd
        def _(eng):
            if not by_src:
                eng.memset(filld[:, :, 0:1], 0.0).then_inc(fill_ready, 1)
                eng.memset(filld[:, :, 1:2], -1.0).then_inc(fill_ready, 1)
                eng.wait_ge(filled, 16)

            def scatter(i, j):
                if by_src:
                    short = isinstance(i, int) and 2 * i + j == NG - 1 and full
                    eng.wait_ge(ea_in[j], (i + 1) * 16 + (16 if short else 0))
                eng.wait_ge(idx_ready[j], i + 1)
                eng.sem_inc(begun, 1)
                for k in range(K):
                    eng.indirect_dma_start(
                        out=table, out_offset=bass.IndirectOffsetOnAxis(ap=idx[j][:, k:k + 1], axis=0),
                        in_=rows[j][:, k, :], in_offset=None).then_inc(sent[j], 16)

            def alone(i):
                for j in range(2):
                    scatter(i, j)

            rounds(eng, n_sort, alone)
            for j in range(2):
                eng.wait_ge(sent[j], n_sort * 16 * K)

        @block.vector
        def _(eng):
            steps = 6

            def hots(i, j):
                g = (2 * i + j) * K
                wait(eng, (oh_used if by_src else ranked)[j], i)
                for s in range(1 + by_src):
                    eng.tensor_tensor(
                        oh[j][:, s, 0:K, :], m["io50"][:, None, :].to_broadcast([P, K, HB]),
                        m["hib"][:, s if by_src else n, span(g, K)][:, :, None].to_broadcast([P, K, HB]),
                        ALU.is_equal).then_inc(oh_ready[j], 1)
                if by_src:
                    eng.tensor_tensor(
                        ohlo[j][:, :, :], m["io128b"][:, None, :].to_broadcast([P, K, P]),
                        lob[:, span(g, K)][:, :, None].to_broadcast([P, K, P]),
                        ALU.is_equal).then_inc(oh_ready[j], 1)

            def rank(i, j, between=None):
                g = (2 * i + j) * K
                step = Count()

                def own(ins, k):
                    ins.then_inc(v, step.up() and 1)
                    if between:
                        between(k)
                    eng.wait_ge(v, (i * 2 + j) * steps + step.n)

                wait(eng, sent[j], i * 16 * K)
                if by_src:
                    eng.tensor_copy(rows[j][:, :, D], m["nlo"][:, span(g, K)])
                    eng.tensor_copy(rows[j][:, :, D + 1].bitcast(i32), m["val"][:, 0, span(g, K)])
                else:
                    eng.tensor_copy(rows[j][:, :, 0].bitcast(i32), m["val"][:, 1, span(g, K)])
                    eng.tensor_copy(rows[j][:, :, 1], m["lo"][:, span(g, K)])
                eng.wait_ge(ranked[j], i + 1)
                own(eng.tensor_tensor(
                    ranks[:, :, :], psr[j][:, 0:K * HB].rearrange("p (k h) -> p k h", h=HB),
                    m["base"][:, n, None, :].to_broadcast([P, K, HB]), ALU.add), 0)
                eng.tensor_tensor(m["base"][:, n, :], m["base"][:, n, :],
                                  psr[j][:, K * HB:(K + 1) * HB], ALU.add).then_inc(summed[j], 1)
                own(eng.tensor_tensor(ranks[:, :, :], ranks[:, :, :], oh[j][:, 0, 0:K, :], ALU.mult), 1)
                own(eng.tensor_reduce(posf[:, :], ranks[:, :, :], AX.X, ALU.add), 2)
                own(eng.tensor_copy(posi[:, :], posf[:, :]), 3)
                eng.tensor_scalar(lane[:, :], posi[:, :], P - 1, None, ALU.bitwise_and).then_inc(v, step.up() and 1)
                own(eng.tensor_scalar(tile[:, :], posi[:, :], 7, None, ALU.arith_shift_right), 4)
                assert step.n == steps
                eng.scalar_tensor_tensor(idx[j][:, :], lane[:, :], float(z.TT), tile[:, :], ALU.mult, ALU.add)\
                   .then_inc(idx_ready[j], 1)

            def codes(i, a):
                o, c = before(i, a, 2, GB)
                eng.wait_ge(pair_in[a], (i + 1) * 16)
                wait(eng, cols_ready[o], c)
                eng.tensor_scalar(code[a % 2][:, :], pair[a][:, :, 1], m["codes"][:, span(i * GB + a, 1)], None,
                                  ALU.subtract).then_inc(code_ready[a], 1)

            def column(i, a, k):
                o, c = before(i, a, 2, GB)
                if k == 0:
                    wait(eng, built[o], c)
                    eng.wait_ge(code_ready[a], i + 1)
                ins = eng.tensor_scalar(one_c[a % 2][:, k, :], m["io784"][:, :], code[a % 2][:, k:k + 1], None,
                                        ALU.is_equal)
                if k == GT - 1:
                    ins.then_inc(cols_ready[a], 1)

            def adj(i, a):
                codes(i, a)
                for k in range(GT):
                    column(i, a, k)

            for j in range(2):
                eng.memset(oh[j][:, :, K, :], 0.0).then_inc(cleared, 1)
            if by_src:
                eng.tensor_copy(lob[:, :], m["lo"][:, :]).then_inc(lob_ready, 1)
                eng.wait_ge(lob_ready, 1)
                hots(0, 0)

                def together(b):
                    for s in range(4):
                        codes(b, 2 * s)
                        rank(b * 2 + s // 2, s % 2, lambda k: column(b, 2 * s, k))
                        hots(b * 2 + (s + 1) // 2, (s + 1) % 2)
                        adj(b, 2 * s + 1)

                def alone(i):
                    rank(i, 0)
                    hots(i, 1)
                    rank(i, 1)
                    if not (isinstance(i, int) and i == n_sort - 1):
                        hots(i + 1, 0)

                def rest(b):
                    for a in range(GB):
                        adj(b, a)

                rounds(eng, n_both, together)
                rounds(eng, n_sort, alone, 2 * n_both)
                rounds(eng, n_adj, rest, n_both)
                eng.wait_ge(deg_ready, 1)
                eng.tensor_copy(m["deg"][:, :], psd[:, 0:z.NB])
            else:
                def simple(i):
                    for j in range(2):
                        hots(i, j)
                        rank(i, j)
                rounds(eng, n_sort, simple)

        @block.scalar
        def _(eng):
            def places(b, a):
                o, c = before(b, a, 2, GB)
                eng.wait_ge(pair_in[a], (b + 1) * 16)
                wait(eng, built[o], c)
                distances(eng, dist[a % 2], m["io128b"][:, :], lambda k: pair[a][:, k, 0:1]).then_inc(dist_ready, 1)
                eng.wait_ge(dist_ready, b * GB + a + 1)
                near(eng, one_s[a % 2][:, :, :], dist[a % 2]).then_inc(places_ready[a], 1)

            def keep(i, u):
                b = 2 * i + u
                wait(eng, stored[u], i * 16)
                for a in range(GB):
                    eng.wait_ge(built[a], b + 1)
                    for s, (f, w) in enumerate(halves):
                        eng.activation(cnts[u][:, f:f + w, a, :],
                                       psa[a % 2][:, s, 0:w * GD].rearrange("p (t d) -> p t d", d=GD),
                                       ACT.Copy).then_inc(copied[a], 1)
                    if not (isinstance(b, int) and b == n_adj - 1 and a + 2 >= GB):
                        places(*seg(b, a + 2, GB))
                for a in range(GB):
                    eng.wait_ge(copied[a], (b + 1) * 2)
                to = m["adj"][b] if isinstance(b, int) else m["adj"][bass.ds(b, 1)].rearrange("o p c -> (o p) c")
                eng.dma_start(to, cnts[u][:, :, :, :].rearrange("p s g d -> p (s g d)")).then_inc(stored[u], 16)

            if by_src:
                places(0, 0)
                places(0, 1)

                def keep_two(i):
                    for u in range(2):
                        keep(i, u)

                rounds(eng, n_adj // 2, keep_two)
                if n_adj % 2:
                    keep(n_adj // 2, 0)
                for u in range(2):
                    eng.wait_ge(stored[u], (n_adj + 1 - u) // 2 * 16)

        @block.tensor
        def _(eng):
            def products(i, j):
                eng.wait_ge(oh_ready[j], (i + 1) * (3 if by_src else 1))
                wait(eng, summed[j], i)
                eng.matmul(psr[j][:, 0:(K + 1) * HB], m["tri"][:, :],
                           oh[j][:, 0, :, :].rearrange("p k h -> p (k h)"), start=True, stop=False,
                           skip_group_check=True)
                for d in range(1, K + 1):
                    mm = eng.matmul(psr[j][:, d * HB:(K + 1) * HB], m["onesb"][:, :],
                                    oh[j][:, 0, 0:K + 1 - d, :].rearrange("p k h -> p (k h)"),
                                    start=False, stop=(d == K), skip_group_check=True)
                mm.then_inc(ranked[j], 1)
                if by_src:
                    for k in range(K):
                        mm = eng.matmul(psd[:, 0:HB], ohlo[j][:, k, :], oh[j][:, 1, k, :], start=False,
                                        stop=False, skip_group_check=True)
                    mm.then_inc(oh_used[j], 1)

            def adj(i, a):
                r = a % 2
                o, c = before(i, a, 2, GB)
                eng.wait_ge(places_ready[a], i + 1)
                eng.wait_ge(cols_ready[a], i + 1)
                wait(eng, copied[o], c * 2)
                for k in range(GT):
                    for s, (f, w) in enumerate(halves):
                        mm = eng.matmul(psa[r][:, s, 0:w * GD], one_s[r][:, k, :],
                                        one_c[r][:, k, f * GD:(f + w) * GD], start=(k == 0), stop=(k == GT - 1))
                mm.then_inc(built[a], 1)

            eng.wait_ge(cleared, 2)
            if by_src:
                eng.matmul(psd[:, 0:HB], m["onesb"][:, :], oh[0][:, 0, K, :], start=True, stop=False,
                           skip_group_check=True)
            if by_src:
                def together(b):
                    for s in range(4):
                        adj(b, 2 * s)
                        products(b * 2 + (s + 1) // 2, (s + 1) % 2)
                        adj(b, 2 * s + 1)

                def alone(i):
                    products(i, 1)
                    if not (isinstance(i, int) and i == n_sort - 1):
                        products(i + 1, 0)

                def rest(b):
                    for a in range(GB):
                        adj(b, a)

                products(0, 0)
                rounds(eng, n_both, together)
                rounds(eng, n_sort, alone, 2 * n_both)
                rounds(eng, n_adj, rest, n_both)
            else:
                def simple(i):
                    for j in range(2):
                        products(i, j)
                rounds(eng, n_sort, simple)
            if by_src:
                eng.matmul(psd[:, 0:HB], m["onesb"][:, :], oh[0][:, 0, K, :], start=False, stop=True,
                           skip_group_check=True).then_inc(deg_ready, 1)


def chunk_transform(nc, z, ctx, sb, ps, sem, m, name, source, w_sb, w_dma, cols, finish, tail=None):
    xc = sb(ctx, f"{name}_xc", [P, BC, D], fp32)
    xT = sb(ctx, f"{name}_xT", [D, BC * P], fp32)
    psT = [ps(ctx, f"{name}_psT{n}", [P, 512], fp32) for n in range(2)]
    nb = -(-BC * cols // 512)
    psW = [ps(ctx, f"{name}_psW{n}", [P, 512], fp32) for n in range(nb)]
    per = 512 // cols
    copied, turned, turned_sb, times, finished, w_in, begun = (
        sem(ctx, f"{name}_{s}") for s in ("copied", "turned", "evac", "times", "finished", "w_in", "begun"))
    block = ctx.enter_context(nc.Block())
    first = 4
    n_it = z.NB // BC

    @block.sync
    def _(eng):
        w_dma(eng, w_in)
        if tail:
            tail(eng, finished, n_it)

    @block.scalar
    def _(eng):
        def chunk(i):
            wait(eng, turned, i)
            eng.activation(xc[:, :, :].rearrange("p b d -> p (b d)"),
                           source[:, :, :].rearrange("p b d -> p (b d)")[:, span(i * BC * D, BC * D)],
                           ACT.Copy).then_inc(copied, 1)
            eng.wait_ge(turned, i + 1)
            wait(eng, times, i)
            eng.activation(xT[:, 0:first * P], psT[0][0:D, 0:first * P], ACT.Copy)
            eng.activation(xT[:, first * P:BC * P], psT[1][0:D, 0:(BC - first) * P], ACT.Copy).then_inc(turned_sb, 1)

        rounds(eng, n_it, chunk)

    @block.tensor
    def _(eng):
        def chunk(i):
            eng.wait_ge(copied, i + 1)
            wait(eng, turned_sb, i)
            eng.sem_inc(begun, 1)
            for b in range(BC):
                q = 0 if b < first else 1
                o = (b - (first if q else 0)) * P
                mm = eng.transpose(psT[q][0:D, o:o + P], xc[:, b, :], m["ident"][:, :])
            mm.then_inc(turned, 1)
            eng.wait_ge(turned_sb, i + 1)
            wait(eng, finished, i)
            for b in range(BC):
                mm = eng.matmul(psW[b // per][:, b % per * cols:(b % per + 1) * cols], xT[:, b * P:(b + 1) * P],
                                w_sb, start=True, stop=True)
            mm.then_inc(times, 1)

        eng.wait_ge(w_in, 16)
        rounds(eng, n_it, chunk)

    @block.vector
    def _(eng):
        def chunk(i):
            eng.wait_ge(times, i + 1)
            finish(eng, i, psW, finished)

        rounds(eng, n_it, chunk)


def table_stage(nc, z, m, sb, ps, sem, W):
    with ExitStack() as ctx:
        part = sb(ctx, "part", [P, BC * C], fp32)
        v = sem(ctx, "v_tab")
        per = 512 // C * C

        def finish(eng, i, psW, finished):
            def cols(n, q, w):
                return m["P3"][n][:, span(i * (BC * C) + q * per, w)]

            widths = [min(per, BC * C - q * per) for q in range(len(psW))]
            nq = len(psW)
            for q, w in enumerate(widths):
                eng.tensor_copy(cols(0, q, w), psW[q][:, 0:w]).then_inc(v, 1)
            eng.wait_ge(v, i * 4 * nq + nq)
            for q, w in enumerate(widths):
                ins = eng.tensor_tensor(part[:, q * per:q * per + w], psW[q][:, 0:w], cols(0, q, w), ALU.subtract)
                ins.then_inc(v, 1)
            eng.wait_ge(v, i * 4 * nq + 2 * nq)
            for q, w in enumerate(widths):
                eng.tensor_copy(cols(1, q, w), part[:, q * per:q * per + w]).then_inc(v, 1)
            eng.wait_ge(v, i * 4 * nq + 3 * nq)
            for q, w in enumerate(widths):
                eng.tensor_tensor(part[:, q * per:q * per + w], part[:, q * per:q * per + w], cols(1, q, w),
                                  ALU.subtract).then_inc(v, 1)
            eng.wait_ge(v, i * 4 * nq + 4 * nq)
            for q, w in enumerate(widths):
                ins = eng.tensor_copy(cols(2, q, w), part[:, q * per:q * per + w])
            ins.then_inc(finished, 1)

        def w_dma(eng, w_in):
            eng.dma_start(m["Wsb"][:, :], W).then_inc(w_in, 16)

        chunk_transform(nc, z, ctx, sb, ps, sem, m, "tab", m["xn"], m["Wsb"][0:D, :], w_dma, C, finish)


def edge_stage(nc, z, m, sb, ps, sem, att):
    HB, NU = z.HB, z.NU
    n_it = NU // BU
    with ExitStack() as ctx:
        buf = [sb(ctx, f"buf{j}", [P, UT, 2 * D + 2], fp32) for j in range(BU)]
        one = [sb(ctx, f"one{q}", [P, UT, P], bf16) for q in range(PRE)]
        dist = [sb(ctx, f"dist_e{q}", [P, UT - 1, P], bf16) for q in range(PRE)]
        xeT = [sb(ctx, f"xeT{q}", [P, UT * P], fp32) for q in range(2)]
        oneT = [sb(ctx, f"oneT{q}", [P, UT * P], bf16) for q in range(2)]
        lg = [sb(ctx, f"lg{q}", [P, UT * 2 * C], fp32) for q in range(PRE)]
        sp = [sb(ctx, f"sp{q}", [P, UT, 2, H, D], fp32) for q in range(2)]
        attb = sb(ctx, "attb", [P, 2, H, D], fp32)
        junk = [sb(ctx, f"junk{q}", [P, UT * H, 2, D], bf16) for q in range(2)]
        sums = sb(ctx, "sums", [P, BU * UT * H], fp32)
        turned = [ps(ctx, f"turned{q}", [P, 512], fp32) for q in range(2)]
        psx = [t[:, 0:UT * P] for t in turned]
        pso = [t[:, UT * P:UT * P + UT * P // 2].bitcast(bf16) for t in turned]
        pre = [ps(ctx, f"pre{q}", [P, UT, 2, C], fp32) for q in range(PRE)]

        def sems(name, n=BU):
            return [sem(ctx, f"{name}{j}") for j in range(n)]

        row_in, got, lo_kept, one_ready, x_turned, o_turned, x_evac, o_evac, pre_ready, exp_done, ln_done, \
            sp_ready, sp_read, stored = (sems(s) for s in (
                "row_in", "got", "lo_kept", "one_ready", "x_turned", "o_turned", "x_evac", "o_evac",
                "pre_ready", "exp_done", "ln_done", "sp_ready", "sp_read", "stored"))
        att_in = sem(ctx, "att_in")
        dist_ready = sem(ctx, "dist_ready")
        padded = sem(ctx, "padded")
        begun = sem(ctx, "gather_begun")
        kept = sem(ctx, "sums_kept")
        block = ctx.enter_context(nc.Block())
        rows = m["rows"].rearrange("(p t) c -> p t c", p=P)

        def last(i):
            return isinstance(i, int) and i == n_it - 1

        @block.sync
        def _(eng):
            for n in range(2):
                eng.dma_start(attb[:, n, :, :], att[:, :, n * D:(n + 1) * D].to_broadcast([P, H, D]))\
                   .then_inc(att_in, 16)
            def load(i, j):
                wait(eng, x_turned[j], i)
                wait(eng, lo_kept[j], i)
                eng.dma_start(buf[j][:, :, D:2 * D + 2], rows[:, span((i * BU + j) * UT, UT), :])\
                   .then_inc(row_in[j], 16)

            def store(i, j):
                q = j % 2
                eng.wait_ge(sp_ready[j], i + 1)
                eng.dma_start(m["outj"][:, span((i * BU + j) * UT * C, UT * C)].rearrange("p (k c) -> p k c", c=C),
                              sp[q][:, :, 1, :, :].rearrange("p k h d -> p k (h d)")).then_inc(stored[j], 16)

            def body(i):
                for j in range(BU):
                    store(i, j)
                    if not last(i):
                        load(i + 1, j)

            for j in range(BU):
                load(0, j)
            paired_rounds(eng, n_it, body)
            for j in range(BU):
                eng.wait_ge(stored[j], n_it * 16)

        @block.gpsimd
        def _(eng):
            for n in range(3):
                eng.memset(m["P3"][n][:, z.NB * C:HB * C], 0.0).then_inc(padded, 1)

            def gather(i):
                for j in range(BU):
                    eng.wait_ge(row_in[j], (i + 1) * 16)
                    eng.sem_inc(begun, 1)
                    for k in range(UT):
                        eng.indirect_dma_start(
                            out=buf[j][:, k, 0:D], out_offset=None, in_=m["x_in"],
                            in_offset=bass.IndirectOffsetOnAxis(
                                ap=buf[j][:, k, 2 * D + 1:2 * D + 2].bitcast(i32), axis=0)).then_inc(got[j], 16)

            paired_rounds(eng, n_it, gather)

        @block.vector
        def _(eng):
            def places(i, j):
                q = j % PRE
                o, c = before(i, j, PRE, BU)
                eng.wait_ge(row_in[j], (i + 1) * 16)
                wait(eng, o_turned[o], c)
                eng.tensor_scalar(one[q][:, 0, :], m["io128b"][:, :], buf[j][:, 0, 2 * D:2 * D + 1], 0.0,
                                  ALU.add, ALU.is_equal).then_inc(one_ready[j], 1)
                eng.tensor_copy(m["nloA"][:, span((i * BU + j) * UT, UT)], buf[j][:, :, 2 * D]).then_inc(lo_kept[j], 1)

            def finish(i, j):
                q = j % 2
                o, c = before(i, j, 2, BU)
                eng.wait_ge(ln_done[j], i + 1)
                wait(eng, stored[o], c * 16)
                wait(eng, sp_read[o], c)
                eng.scalar_tensor_tensor(sp[q][:, :, :, :, :].rearrange("p k s h d -> p (k s h d)"),
                                         lg[j % PRE][:, :], CAP_SP,
                                         pre[j % PRE][:, :, :, :].rearrange("p k s c -> p (k s c)"),
                                         ALU.min, ALU.max).then_inc(sp_ready[j], 1)
                eng.wait_ge(sp_ready[j], i + 1)
                if j == 0:
                    wait(eng, kept, i)
                for k in range(UT):
                    for h in range(H):
                        n = (j * UT + k) * H + h
                        ins = eng.tensor_tensor_reduce(junk[q][:, k * H + h, :, :], sp[q][:, k, :, h, :],
                                                       attb[:, :, h, :], 1.0, 0.0, ALU.mult, ALU.add,
                                                       sums[:, n:n + 1])
                ins.then_inc(sp_read[j], 1)

            def body(i):
                for j in range(BU):
                    if not (last(i) and j + PRE >= BU):
                        places(*seg(i, j + PRE, BU))
                    finish(i, j)
                eng.wait_ge(sp_read[BU - 1], i + 1)
                w = BU * UT
                eng.tensor_copy(m["alpha"][:, span(i * w, w), :],
                                sums[:, :].rearrange("p (t h) -> p t h", h=H)).then_inc(kept, 1)

            eng.wait_ge(att_in, 32)
            for j in range(PRE):
                places(0, j)
            paired_rounds(eng, n_it, body)

        @block.scalar
        def _(eng):
            def places(i, j):
                q = j % PRE
                o, c = before(i, j, PRE, BU)
                eng.wait_ge(row_in[j], (i + 1) * 16)
                wait(eng, o_turned[o], c)
                distances(eng, dist[q], m["io128b"][:, :], lambda k: buf[j][:, 1, 2 * D:2 * D + 1])\
                    .then_inc(dist_ready, 1)
                eng.wait_ge(dist_ready, i * BU + j + 1)
                near(eng, one[q][:, 1:UT, :], dist[q]).then_inc(one_ready[j], 1)

            def evacuate(i, j):
                q = j % 2
                o, c = before(i, j, 2, BU)
                wait(eng, pre_ready[o], c)
                eng.wait_ge(x_turned[j], i + 1)
                eng.activation(xeT[q][:, :], psx[q], ACT.Copy).then_inc(x_evac[j], 1)
                eng.activation(oneT[q][:, :], pso[q], ACT.Copy).then_inc(o_evac[j], 1)

            def softplus(i, j):
                q = j % PRE
                o, c = before(i, j, PRE, BU)
                eng.wait_ge(pre_ready[j], i + 1)
                wait(eng, sp_ready[o], c)
                eng.activation(lg[q][:, :], pre[q][:, :, :, :].rearrange("p k s c -> p (k s c)"), ACT.Exp)\
                   .then_inc(exp_done[j], 1)
                eng.wait_ge(exp_done[j], i + 1)
                eng.activation(lg[q][:, :], lg[q][:, :], ACT.Ln, bias=1.0).then_inc(ln_done[j], 1)

            def body(i):
                for j in range(BU):
                    if not (last(i) and j + PRE >= BU):
                        places(*seg(i, j + PRE, BU))
                    if not (last(i) and j + 2 >= BU):
                        evacuate(*seg(i, j + 2, BU))
                    if not (last(i) and j + 1 >= BU):
                        softplus(*seg(i, j + 1, BU))

            eng.preload_act_table_set("natural_log_exp_and_others")
            for j in range(PRE):
                places(0, j)
            evacuate(0, 0)
            evacuate(0, 1)
            softplus(0, 0)
            paired_rounds(eng, n_it, body)

        @block.tensor
        def _(eng):
            def turn(i, j):
                q = j % 2
                o, c = before(i, j, 2, BU)
                eng.wait_ge(one_ready[j], (i + 1) * 2)
                wait(eng, o_evac[o], c)
                eng.wait_ge(got[j], (i + 1) * 16 * UT)
                for k in range(UT):
                    mm = eng.transpose(pso[q][:, k * P:(k + 1) * P], one[j % PRE][:, k, :], m["identb"][:, :])
                mm.then_inc(o_turned[j], 1)
                for k in range(UT):
                    mm = eng.transpose(psx[q][:, k * P:(k + 1) * P], buf[j][:, k, 0:2 * D], m["ident"][:, :])
                mm.then_inc(x_turned[j], 1)

            def product(i, j, b):
                q = j % 2
                o, c = before(i, j, PRE, BU)
                eng.wait_ge(o_evac[j], i + 1)
                wait(eng, sp_ready[o], c)
                for k in range(UT):
                    xt = xeT[q][:, k * P:(k + 1) * P]
                    eng.matmul(pre[j % PRE][:, k, 1, :], xt, m["Wsb"][:, :], start=True, stop=True)
                    eng.matmul(pre[j % PRE][:, k, 0, :], xt[D:2 * D, :], m["Wsb"][D:2 * D, :], start=True, stop=False,
                               skip_group_check=True)
                    for n in range(3):
                        mm = eng.matmul(pre[j % PRE][:, k, 0, :], oneT[q][:, k * P:(k + 1) * P],
                                        m["P3"][n][:, bass.ds(b * C, C)], start=False, stop=(n == 2),
                                        skip_group_check=True)
                mm.then_inc(pre_ready[j], 1)

            def body(i):
                for j in range(BU):
                    b = eng.value_load(m["blkS"][0:1, 0, span(i * BU + j, 1)], min_val=0, max_val=HB - 1)
                    if not (last(i) and j + 1 >= BU):
                        turn(*seg(i, j + 1, BU))
                    product(i, j, b)

            eng.wait_ge(padded, 3)
            turn(0, 0)
            paired_rounds(eng, n_it, body)


def newton_rsqrt(eng, v, c, a, y, t):
    eng.tensor_tensor(t, y, y, ALU.mult).then_inc(v, c.up() and 1)
    eng.wait_ge(v, c.n)
    eng.tensor_tensor(t, t, a, ALU.mult).then_inc(v, c.up() and 1)
    eng.wait_ge(v, c.n)
    eng.tensor_scalar(t, t, -0.5, 1.5, ALU.mult, ALU.add).then_inc(v, c.up() and 1)
    eng.wait_ge(v, c.n)
    eng.tensor_tensor(y, y, t, ALU.mult).then_inc(v, c.up() and 1)
    eng.wait_ge(v, c.n)


def softmax_stage(nc, z, m, sb, ps, sem, gamma, beta):
    TT = z.TT
    A = m["alpha"]
    with ExitStack() as ctx:
        t1 = sb(ctx, "t1", [P, TT, H], fp32)
        mask = sb(ctx, "mask", [P, TT], fp32)
        msum = sb(ctx, "msum", [P, H], fp32)
        mu = sb(ctx, "mu", [P, H], fp32)
        sq = sb(ctx, "sq", [P, H], fp32)
        var = sb(ctx, "var", [P, H], fp32)
        rs = sb(ctx, "rs", [P, H], fp32)
        tt = sb(ctx, "tt", [P, H], fp32)
        pmax = sb(ctx, "pmax", [P, H], fp32)
        gmax = sb(ctx, "gmax", [H, 1], fp32)
        dg = sb(ctx, "dg", [H, H], fp32)
        far = sb(ctx, "far", [P, 1], fp32)
        gb = sb(ctx, "gb", [P, 2, H], fp32)
        psS = [ps(ctx, f"psS{n}", [P, 512], fp32) for n in range(4)]
        v = sem(ctx, "v_sm")
        ln_ready = sem(ctx, "sm_ln")
        exp_done = sem(ctx, "sm_exp")
        par_in = sem(ctx, "par_in")
        sums_ready, squares_ready, var_ready, root_ready, capped, maxima, diag, shifted = (
            sem(ctx, f"sm_{s}") for s in ("sums", "squares", "var", "root", "capped", "maxima", "diag", "shifted"))
        across = sem(ctx, "sm_across")
        block = ctx.enter_context(nc.Block())

        def flat(t):
            return t[:, :, :].rearrange("p t h -> p (t h)")

        def by_head(t):
            return t[:, :, :].rearrange("p t h -> p h t")

        def all_tiles(x):
            return x[:, None, :].to_broadcast([P, TT, H])

        maskb = mask[:, :, None].to_broadcast([P, TT, H])

        @block.sync
        def _(eng):
            for n, g in enumerate((gamma, beta)):
                eng.dma_start(gb[:, n, :], g.rearrange("(o h) -> o h", o=1).to_broadcast([P, H])).then_inc(par_in, 16)

        @block.scalar
        def _(eng):
            eng.preload_act_table_set("natural_log_exp_and_others")
            eng.wait_ge(capped, 1)
            eng.activation(flat(t1), flat(t1), ACT.Exp).then_inc(exp_done, 1)
            eng.wait_ge(exp_done, 1)
            eng.activation(flat(t1), flat(t1), ACT.Ln, bias=1.0).then_inc(ln_ready, 1)
            eng.wait_ge(var_ready, 1)
            eng.activation(rs[:, :], var[:, :], ACT.Sqrt).then_inc(root_ready, 1)
            eng.wait_ge(capped, 2)
            eng.activation(flat(t1), flat(t1), ACT.Exp).then_inc(exp_done, 1)
            eng.wait_ge(exp_done, 2)
            eng.activation(flat(t1), flat(t1), ACT.Ln, bias=1.0).then_inc(ln_ready, 1)

        @block.tensor
        def _(eng):
            eng.wait_ge(sums_ready, 1)
            eng.matmul(psS[0][:, 0:H], m["onesf"][:, :], msum[:, :], start=True, stop=True).then_inc(across, 1)
            eng.wait_ge(squares_ready, 1)
            eng.matmul(psS[1][:, 0:H], m["onesf"][:, :], sq[:, :], start=True, stop=True).then_inc(across, 1)
            eng.wait_ge(maxima, 1)
            eng.transpose(psS[2][0:H, 0:P], pmax[:, :], m["ident"][:, :]).then_inc(across, 1)
            eng.wait_ge(diag, 1)
            eng.matmul(psS[3][:, 0:H], m["onesf"][0:H, :], dg[:, :], start=True, stop=True).then_inc(across, 1)
            eng.wait_ge(shifted, 1)
            eng.matmul(psS[0][:, 64:65], m["onesf"][:, :], far[:, :], start=True, stop=True).then_inc(across, 1)

        @block.vector
        def _(eng):
            c = Count()

            def done(ins):
                ins.then_inc(v, c.up() and 1)
                eng.wait_ge(v, c.n)

            eng.tensor_scalar(flat(t1), flat(A), CAP_SP, None, ALU.min).then_inc(capped, 1)
            done(eng.tensor_scalar(mask[:, :], m["nloA"][:, :], 0.0, None, ALU.is_le))
            eng.wait_ge(ln_ready, 1)
            done(eng.scalar_tensor_tensor(flat(A), flat(t1), CAP_SP, flat(A), ALU.min, ALU.max))
            done(eng.tensor_tensor(t1[:, :, :], A[:, :, :], maskb, ALU.mult))
            eng.tensor_reduce(msum[:, :], by_head(t1), AX.X, ALU.add).then_inc(sums_ready, 1)
            eng.wait_ge(across, 1)
            done(eng.tensor_scalar(mu[:, :], psS[0][:, 0:H], 1.0 / z.E, None, ALU.mult))
            done(eng.tensor_tensor(A[:, :, :], A[:, :, :], all_tiles(mu), ALU.subtract))
            done(eng.tensor_tensor(t1[:, :, :], A[:, :, :], maskb, ALU.mult))
            done(eng.tensor_tensor(t1[:, :, :], t1[:, :, :], A[:, :, :], ALU.mult))
            eng.tensor_reduce(sq[:, :], by_head(t1), AX.X, ALU.add).then_inc(squares_ready, 1)
            eng.wait_ge(across, 2)
            eng.tensor_scalar(var[:, :], psS[1][:, 0:H], 1.0 / z.E, BN_EPS, ALU.mult, ALU.add).then_inc(var_ready, 1)
            eng.wait_ge(root_ready, 1)
            done(eng.reciprocal(rs[:, :], rs[:, :]))
            newton_rsqrt(eng, v, c, var[:, :], rs[:, :], tt[:, :])
            eng.wait_ge(par_in, 32)
            done(eng.tensor_tensor(rs[:, :], rs[:, :], gb[:, 0, :], ALU.mult))
            done(eng.tensor_tensor(A[:, :, :], A[:, :, :], all_tiles(rs), ALU.mult))
            done(eng.tensor_tensor(A[:, :, :], A[:, :, :], gb[:, 1, None, :].to_broadcast([P, TT, H]), ALU.add))
            eng.tensor_scalar(flat(t1), flat(A), CAP_SP, None, ALU.min).then_inc(capped, 1)
            eng.wait_ge(ln_ready, 2)
            done(eng.scalar_tensor_tensor(flat(A), flat(t1), CAP_SP, flat(A), ALU.min, ALU.max))
            done(eng.tensor_tensor(A[:, :, :], A[:, :, :], maskb, ALU.mult))
            eng.tensor_reduce(pmax[:, :], by_head(A), AX.X, ALU.max).then_inc(maxima, 1)
            eng.wait_ge(across, 3)
            done(eng.tensor_reduce(gmax[:, :], psS[2][0:H, 0:P], AX.X, ALU.max))
            eng.tensor_scalar(dg[:, :], m["ident"][0:H, 0:H], gmax[:, 0:1], None, ALU.mult).then_inc(diag, 1)
            eng.wait_ge(across, 4)
            done(eng.tensor_copy(m["top"][:, :], psS[3][:, 0:H]))
            done(eng.tensor_scalar(tt[:, :], m["top"][:, :], -RANGE, None, ALU.add))
            done(eng.tensor_tensor(t1[:, :, :], A[:, :, :], all_tiles(tt), ALU.is_lt))
            done(eng.tensor_tensor(t1[:, :, :], t1[:, :, :], maskb, ALU.mult))
            eng.tensor_reduce(far[:, :], flat(t1), AX.X, ALU.add).then_inc(shifted, 1)
            eng.wait_ge(across, 5)
            eng.tensor_scalar(m["flag"][0:1, 1:2], psS[0][0:1, 64:65], 0.0, None, ALU.is_gt)


def node_max_stage(nc, z, m, sb, ps, sem):
    A = m["alpha"]
    with ExitStack() as ctx:
        mx = sb(ctx, "mx", [P, z.HB, H], fp32)
        pick = sb(ctx, "pick", [P, H, P], fp32)
        tmax = sb(ctx, "tmax", [P, H], fp32)
        hot = sb(ctx, "hotm", [P, P], fp32)
        hotT = sb(ctx, "hotT", [P, P], fp32)
        psp = ps(ctx, "psp", [P, H, P], fp32)
        psm = ps(ctx, "pslook", [P, 512], fp32)
        cleared, picked, turned, taken, maxed = (sem(ctx, f"nm_{s}") for s in (
            "cleared", "picked", "turned", "taken", "maxed"))
        hot_ready, hot_turned, hot_kept, looked_up, off = (sem(ctx, f"nm_{s}") for s in (
            "hot", "hot_turned", "hot_kept", "looked_up", "off"))
        loA = sb(ctx, "loA", [P, z.TT], fp32)
        lo_ready = sem(ctx, "nm_lo")
        block = ctx.enter_context(nc.Block())

        @block.gpsimd
        def _(eng):
            eng.memset(mx[:, :, :], 0.0).then_inc(cleared, 1)

        @block.sync
        def _(eng):
            eng.wait_ge(off, z.TT)

        @block.scalar
        def _(eng):
            def keep(i):
                for k in range(UT):
                    t = i * UT + k
                    eng.wait_ge(hot_turned, t + 1)
                    eng.activation(hotT[:, :], psp[:, 0, :], ACT.Copy).then_inc(hot_kept, 1)

            rounds(eng, z.NU, keep)

        @block.vector
        def _(eng):
            def block_of(i, k):
                return eng.value_load(m["blkS"][0:1, 0, span(i, 1)], min_val=0, max_val=z.HB - 1)

            def maxima(i):
                b = block_of(i, 0)
                for k in range(UT):
                    t = i * UT + k
                    for h in range(H):
                        ins = eng.tensor_scalar(pick[:, h, :], m["io128"][:, :], loA[:, span(t, 1)],
                                                A[:, span(t, 1), h], ALU.is_equal, ALU.mult)
                    ins.then_inc(picked, 1)
                    eng.wait_ge(turned, t + 1)
                    eng.tensor_reduce(tmax[:, :], psp[:, :, :], AX.X, ALU.max).then_inc(taken, 1)
                    eng.wait_ge(taken, t + 1)
                    a = mx[:, bass.ds(b, 1), :].rearrange("p o h -> p (o h)")
                    eng.tensor_tensor(a, a, tmax[:, :], ALU.max).then_inc(maxed, 1)
                    eng.wait_ge(maxed, t + 1)

            def take_off(i):
                for k in range(UT):
                    t = i * UT + k
                    eng.tensor_scalar(hot[:, :], m["io128"][:, :], loA[:, span(t, 1)], None,
                                      ALU.is_equal).then_inc(hot_ready, 1)
                    eng.wait_ge(looked_up, t + 1)
                    a = A[:, span(t, 1), :].rearrange("p o h -> p (o h)")
                    eng.tensor_tensor(a, a, psm[:, 0:H], ALU.subtract).then_inc(off, 1)

            eng.tensor_scalar(loA[:, :], m["nloA"][:, :], -1.0, None, ALU.mult).then_inc(lo_ready, 1)
            eng.wait_ge(lo_ready, 1)
            eng.wait_ge(cleared, 1)
            rounds(eng, z.NU, maxima)
            rounds(eng, z.NU, take_off)
            eng.wait_ge(off, z.TT)
            eng.memset(m["top"][:, :], 0.0)

        @block.tensor
        def _(eng):
            def turn(i):
                for k in range(UT):
                    t = i * UT + k
                    eng.wait_ge(picked, t + 1)
                    for h in range(H):
                        mm = eng.transpose(psp[:, h, :], pick[:, h, :], m["ident"][:, :])
                    mm.then_inc(turned, 1)

            def look_up(i):
                b = eng.value_load(m["blkS"][0:1, 0, span(i, 1)], min_val=0, max_val=z.HB - 1)
                for k in range(UT):
                    t = i * UT + k
                    eng.wait_ge(hot_ready, t + 1)
                    eng.transpose(psp[:, 0, :], hot[:, :], m["ident"][:, :]).then_inc(hot_turned, 1)
                    eng.wait_ge(hot_kept, t + 1)
                    eng.matmul(psm[:, 0:H], hotT[:, :], mx[:, bass.ds(b, 1), :].rearrange("p o h -> p (o h)"),
                               start=True, stop=True).then_inc(looked_up, 1)

            rounds(eng, z.NU, turn)
            rounds(eng, z.NU, look_up)


def weight_stage(nc, z, m, sb, ps, sem):
    A = m["alpha"]
    with ExitStack() as ctx:
        mask = sb(ctx, "wmask", [P, z.TT], fp32)
        v, shifted, exp_done = sem(ctx, "v_w"), sem(ctx, "w_shifted"), sem(ctx, "w_exp")
        block = ctx.enter_context(nc.Block())
        flat = A[:, :, :].rearrange("p t h -> p (t h)")

        @block.scalar
        def _(eng):
            eng.wait_ge(shifted, 1)
            eng.activation(flat, flat, ACT.Exp).then_inc(exp_done, 1)

        @block.vector
        def _(eng):
            eng.tensor_scalar(mask[:, :], m["nloA"][:, :], 0.0, None, ALU.is_le).then_inc(v, 1)
            eng.tensor_tensor(A[:, :, :], A[:, :, :], m["top"][:, None, :].to_broadcast([P, z.TT, H]),
                              ALU.subtract).then_inc(shifted, 1)
            eng.wait_ge(v, 1)
            eng.wait_ge(exp_done, 1)
            eng.tensor_tensor(A[:, :, :], A[:, :, :], mask[:, :, None].to_broadcast([P, z.TT, H]), ALU.mult)


def message_stage(nc, z, m, sb, ps, sem):
    n_it = z.NU // BU
    with ExitStack() as ctx:
        oj = [sb(ctx, f"oj{j}", [P, UT, H, D], fp32) for j in range(BU)]
        ND = BU
        msg = [sb(ctx, f"msg{q}", [P, UT, C + H], fp32) for q in range(ND)]
        one = [sb(ctx, f"onem{q}", [P, UT, P], fp32) for q in range(ND)]
        psm = [ps(ctx, f"psm{q}", [P, 512], fp32) for q in range(BU)]
        dist = [sb(ctx, f"dist_m{q}", [P, UT, P], fp32) for q in range(ND)]
        dist_ready = sem(ctx, "distm_ready")
        one_ready = [sem(ctx, f"onem_ready{j}") for j in range(BU)]
        oj_in, oj_used, weights_ready, summed, added = ([sem(ctx, f"{s}{j}") for j in range(BU)] for s in (
            "oj_in", "oj_used", "weights_ready", "msg_summed", "msg_added"))
        cleared = sem(ctx, "acc_zero")
        block = ctx.enter_context(nc.Block())

        def last(i):
            return isinstance(i, int) and i == n_it - 1

        @block.sync
        def _(eng):
            def load(i):
                for j in range(BU):
                    wait(eng, oj_used[j], i)
                    eng.dma_start(oj[j][:, :, :, :].rearrange("p k h d -> p (k h d)"),
                                  m["outj"][:, span((i * BU + j) * UT * C, UT * C)]).then_inc(oj_in[j], 16)

            paired_rounds(eng, n_it, load)

        @block.gpsimd
        def _(eng):
            eng.memset(m["acc"][:, :, :], 0.0).then_inc(cleared, 1)

        @block.scalar
        def _(eng):
            def away(i, j):
                o, c = before(i, j, ND, BU)
                wait(eng, summed[o], c)
                distances(eng, dist[j % ND], m["io128"][:, :],
                          lambda k: m["nloA"][:, span((i * BU + j) * UT + k, 1)]).then_inc(dist_ready, 1)

            def body(i):
                for j in range(BU):
                    if not (last(i) and j + 1 >= BU):
                        away(*seg(i, j + 1, BU))
                    eng.wait_ge(dist_ready, i * BU + j + 1)
                    near(eng, one[j % ND][:, :, :], dist[j % ND]).then_inc(one_ready[j], 1)
                    eng.copy(msg[j % ND][:, :, C:C + H], m["alpha"][:, span((i * BU + j) * UT, UT), :])\
                       .then_inc(weights_ready[j], 1)

            away(0, 0)
            paired_rounds(eng, n_it, body)

        @block.vector
        def _(eng):
            def product(i, j):
                q = j % ND
                o, c = before(i, j, ND, BU)
                t = (i * BU + j) * UT
                eng.wait_ge(oj_in[j], (i + 1) * 16)
                wait(eng, summed[o], c)
                eng.tensor_tensor(msg[q][:, :, 0:C].rearrange("p k (h d) -> p k h d", h=H), oj[j][:, :, :, :],
                                  m["alpha"][:, span(t, UT), :][:, :, :, None].to_broadcast([P, UT, H, D]),
                                  ALU.mult).then_inc(oj_used[j], 1)

            def add(i, j, b):
                eng.wait_ge(summed[j], i + 1)
                o, c = before(i, j, 1, BU)
                wait(eng, added[o], c)
                a = m["acc"][:, bass.ds(b, 1), :].rearrange("p o c -> p (o c)")
                eng.tensor_tensor(a, a, psm[j][:, 0:C + H], ALU.add).then_inc(added[j], 1)

            def body(i):
                for j in range(BU):
                    b = eng.value_load(m["blkS"][0:1, 0, span(i * BU + j, 1)], min_val=0, max_val=z.HB - 1)
                    if not (last(i) and j + 2 >= BU):
                        product(*seg(i, j + 2, BU))
                    add(i, j, b)

            eng.wait_ge(cleared, 1)
            product(0, 0)
            product(0, 1)
            paired_rounds(eng, n_it, body)

        @block.tensor
        def _(eng):
            def sums(i):
                for j in range(BU):
                    q = j % ND
                    eng.wait_ge(one_ready[j], i + 1)
                    eng.wait_ge(oj_used[j], i + 1)
                    eng.wait_ge(weights_ready[j], i + 1)
                    wait(eng, added[j], i)
                    for k in range(UT):
                        mm = eng.matmul(psm[j][:, 0:C + H], one[q][:, k, :], msg[q][:, k, :], start=(k == 0),
                                        stop=(k == UT - 1))
                    mm.then_inc(summed[j], 1)

            paired_rounds(eng, n_it, sums)


class Norm:

    def __init__(self, z, ctx, sb, sem, name):
        self.z = z
        self.d2 = sb(ctx, f"{name}_d2", [P, z.NB, D], fp32)
        self.mean, self.var, self.rs, self.tt = (
            sb(ctx, f"{name}_{s}", [P, z.NB], fp32) for s in ("mean", "var", "rs", "tt"))
        self.var_ready, self.root_ready = sem(ctx, f"{name}_var"), sem(ctx, f"{name}_root")

    def scalar(self, eng):
        eng.wait_ge(self.var_ready, 1)
        eng.activation(self.rs[:, :], self.var[:, :], ACT.Sqrt).then_inc(self.root_ready, 1)

    def vector(self, eng, a, out, v, c):
        def done(ins):
            ins.then_inc(v, c.up() and 1)
            eng.wait_ge(v, c.n)

        def bc(x):
            return x[:, :, None].to_broadcast([P, self.z.NB, D])

        done(eng.tensor_reduce(self.mean[:, :], a, AX.X, ALU.add))
        done(eng.tensor_scalar(self.mean[:, :], self.mean[:, :], 1.0 / D, None, ALU.mult))
        done(eng.tensor_tensor(a, a, bc(self.mean), ALU.subtract))
        done(eng.tensor_tensor(self.d2[:, :, :], a, a, ALU.mult))
        done(eng.tensor_reduce(self.var[:, :], self.d2[:, :, :], AX.X, ALU.add))
        eng.tensor_scalar(self.var[:, :], self.var[:, :], 1.0 / D, LN_EPS, ALU.mult, ALU.add)\
           .then_inc(self.var_ready, 1)
        eng.wait_ge(self.root_ready, 1)
        done(eng.reciprocal(self.rs[:, :], self.rs[:, :]))
        newton_rsqrt(eng, v, c, self.var[:, :], self.rs[:, :], self.tt[:, :])
        done(eng.tensor_tensor(out, a, bc(self.rs), ALU.mult))


def node_stage(nc, z, m, sb, ps, sem, bias):
    NB = z.NB
    acc = m["acc"]
    with ExitStack() as ctx:
        rec = sb(ctx, "rec", [P, NB, H], fp32)
        bb = sb(ctx, "bb", [P, D], fp32)
        prod = sb(ctx, "prod", [P, NB, D], fp32)
        norm = Norm(z, ctx, sb, sem, "ln0")
        v, bias_in = sem(ctx, "v_node"), sem(ctx, "bias_in")
        block = ctx.enter_context(nc.Block())

        @block.sync
        def _(eng):
            eng.dma_start(bb[:, :], bias.rearrange("(o d) -> o d", o=1).to_broadcast([P, D])).then_inc(bias_in, 16)

        @block.scalar
        def _(eng):
            norm.scalar(eng)

        @block.vector
        def _(eng):
            c = Count()

            def done(ins):
                ins.then_inc(v, c.up() and 1)
                eng.wait_ge(v, c.n)

            done(eng.tensor_scalar(rec[:, :, :], acc[:, 0:NB, C:C + H], float(H), 1e-37, ALU.mult, ALU.max))
            done(eng.reciprocal(rec[:, :, :], rec[:, :, :]))
            eng.wait_ge(bias_in, 16)
            x = m["xn"][:, :, :]
            done(eng.tensor_tensor(x, x, bb[:, None, :].to_broadcast([P, NB, D]), ALU.add))
            for h in range(H):
                done(eng.tensor_tensor(prod[:, :, :], acc[:, 0:NB, h * D:(h + 1) * D],
                                       rec[:, :, h, None].to_broadcast([P, NB, D]), ALU.mult))
                done(eng.tensor_tensor(x, x, prod[:, :, :], ALU.add))
            norm.vector(eng, x, x, v, c)


def transform_stage(nc, z, m, sb, ps, sem, n, w):
    with ExitStack() as ctx:
        wsb = sb(ctx, f"w{n}sb", [D, D], fp32)
        source = m["xn"] if n == 0 else m["hn"]

        def finish(eng, i, psW, finished):
            eng.tensor_tensor(m["gs"][:, span(i * BC, BC), :], psW[0][:, 0:BC * D].rearrange("p (b d) -> p b d", d=D),
                              m["dinv"][:, span(i * BC, BC)][:, :, None].to_broadcast([P, BC, D]),
                              ALU.mult).then_inc(finished, 1)

        def w_dma(eng, w_in):
            eng.dma_start(wsb[:, :], w).then_inc(w_in, 16)

        chunk_transform(nc, z, ctx, sb, ps, sem, m, f"tr{n}", source, wsb[:, :], w_dma, D, finish)


def degree_stage(nc, z, m, sb, ps, sem):
    with ExitStack() as ctx:
        tt = sb(ctx, "dtt", [P, z.NB], fp32)
        many = sb(ctx, "many", [P, z.NB], fp32)
        most = sb(ctx, "most", [P, 1], fp32)
        psb = ps(ctx, "psb", [P, 512], fp32)
        v, ready, root = sem(ctx, "v_deg"), sem(ctx, "deg_plus"), sem(ctx, "deg_root")
        bad_ready, bad_sum = sem(ctx, "bad_ready"), sem(ctx, "bad_sum")
        block = ctx.enter_context(nc.Block())

        @block.scalar
        def _(eng):
            eng.wait_ge(ready, 1)
            eng.activation(m["dinv"][:, :], m["deg"][:, :], ACT.Sqrt).then_inc(root, 1)

        @block.tensor
        def _(eng):
            eng.wait_ge(bad_ready, 1)
            eng.matmul(psb[:, 0:1], m["onesf"][:, :], m["bad"][:, :], start=True, stop=True).then_inc(bad_sum, 1)

        @block.vector
        def _(eng):
            c = Count()

            def done(ins):
                ins.then_inc(v, c.up() and 1)
                eng.wait_ge(v, c.n)

            done(eng.tensor_scalar(many[:, :], m["deg"][:, :], float(EXACT), None, ALU.is_gt))
            done(eng.tensor_reduce(most[:, :], many[:, :], AX.X, ALU.max))
            eng.tensor_tensor(m["bad"][:, :], m["bad"][:, :], most[:, :], ALU.add).then_inc(bad_ready, 1)
            eng.tensor_scalar(m["deg"][:, :], m["deg"][:, :], 1.0, None, ALU.add).then_inc(ready, 1)
            eng.wait_ge(root, 1)
            done(eng.reciprocal(m["dinv"][:, :], m["dinv"][:, :]))
            newton_rsqrt(eng, v, c, m["deg"][:, :], m["dinv"][:, :], tt[:, :])
            eng.wait_ge(bad_sum, 1)
            eng.tensor_scalar(m["flag"][0:1, 0:1], psb[0:1, 0:1], 0.0, None, ALU.is_gt)


def dense_stage(nc, z, m, sb, ps, sem, n):
    NB, NS = z.NB, BC
    with ExitStack() as ctx:
        parts = sb(ctx, f"parts{n}", [P, NB, 3, D], bf16)
        rest = m["agg"][:, 0:NB, :]
        adj = [sb(ctx, f"adj{n}{j}", [P, NB, P], bf16) for j in range(NS)]
        psz = [ps(ctx, f"psz{n}{j}", [P, 512], fp32) for j in range(NS)]
        v = sem(ctx, f"v_dense{n}")
        adj_in, summed, kept = ([sem(ctx, f"{s}{n}_{j}") for j in range(NS)] for s in ("adj_in", "z_summed", "z_kept"))
        block = ctx.enter_context(nc.Block())

        @block.sync
        def _(eng):
            def load(i):
                for j in range(NS):
                    wait(eng, summed[j], i)
                    b = i * NS + j
                    a = m["adj"][b] if isinstance(b, int) else m["adj"][bass.ds(b, 1)].rearrange("o p c -> (o p) c")
                    eng.dma_start(adj[j][:, :, :].rearrange("p s d -> p (s d)"), a).then_inc(adj_in[j], 16)

            rounds(eng, NB // NS, load)

        @block.vector
        def _(eng):
            c = Count()

            def done(ins):
                ins.then_inc(v, c.up() and 1)
                eng.wait_ge(v, c.n)

            done(eng.tensor_copy(parts[:, :, 0, :], m["gs"][:, :, :]))
            done(eng.tensor_tensor(rest, m["gs"][:, :, :], parts[:, :, 0, :], ALU.subtract))
            done(eng.tensor_copy(parts[:, :, 1, :], rest))
            done(eng.tensor_tensor(rest, rest, parts[:, :, 1, :], ALU.subtract))
            done(eng.tensor_copy(parts[:, :, 2, :], rest))

            def keep(i):
                for j in range(NS):
                    eng.wait_ge(summed[j], i + 1)
                    eng.tensor_reduce(m["agg"][:, span(i * NS + j, 1), :].rearrange("p o d -> p (o d)"),
                                      psz[j][:, 0:3 * D].rearrange("p (r d) -> p d r", r=3), AX.X, ALU.add)\
                       .then_inc(kept[j], 1)

            rounds(eng, NB // NS, keep)

        @block.tensor
        def _(eng):
            eng.wait_ge(v, 5)

            def products(i):
                for j in range(NS):
                    eng.wait_ge(adj_in[j], (i + 1) * 16)
                    wait(eng, kept[j], i)
                    for s in range(NB):
                        mm = eng.matmul(psz[j][:, 0:3 * D], adj[j][:, s, :],
                                        parts[:, s, :, :].rearrange("p r d -> p (r d)"), start=(s == 0),
                                        stop=(s == NB - 1))
                    mm.then_inc(summed[j], 1)

            rounds(eng, NB // NS, products)


def gather_stage(nc, z, m, sb, ps, sem, n):
    n_it = z.NU // BU
    with ExitStack() as ctx:
        wrote = sem(ctx, f"wrote{n}")
        rd = sb(ctx, f"rd{n}", [P, z.TT, 2], fp32)
        idx = [sb(ctx, f"gidx{n}{q}", [P, BU * UT], i32) for q in range(2)]
        g = [sb(ctx, f"gx{n}{q}", [P, UT, D], fp32) for q in range(2 * BU)]
        one = [sb(ctx, f"oneg{n}{q}", [P, UT, P], fp32) for q in range(2)]
        psg = [ps(ctx, f"psg{n}{q}", [P, 512], fp32) for q in range(BU)]
        NS = 2 * BU
        rd_in, cleared, begun = sem(ctx, f"rd_in{n}"), sem(ctx, f"agg_zero{n}"), sem(ctx, f"begun{n}")
        idx_ready = [sem(ctx, f"gidx_ready{n}{q}") for q in range(2)]
        got, one_ready, summed, added = ([sem(ctx, f"{s}{n}_{j}") for j in range(NS)] for s in (
            "g_got", "g_one", "g_summed", "g_added"))
        block = ctx.enter_context(nc.Block())
        assert n_it % 2 == 1

        def bodies(eng, emit):
            def pair(i):
                for a in range(2):
                    emit(i, a)
            rounds(eng, n_it // 2, pair)
            emit(n_it // 2, 0)

        @block.sync
        def _(eng):
            eng.dma_start(m["gtab"][n].rearrange("(b p) d -> p b d", p=P), m["gs"][:, :, :]).then_inc(wrote, 16)
            eng.dma_start(rd[:, :, :], m["rows_d"].rearrange("(p t) c -> p t c", p=P)).then_inc(rd_in, 16)
            eng.wait_ge(wrote, 16)

        @block.scalar
        def _(eng):
            eng.wait_ge(rd_in, 16)

            def emit(i, a):
                for j in range(BU):
                    wait(eng, got[a * BU + j], i * 16 * UT)
                t = (2 * i + a) * BU * UT
                eng.copy(idx[a][:, :], rd[:, span(t, BU * UT), 0].bitcast(i32)).then_inc(idx_ready[a], 1)

            bodies(eng, emit)

        @block.gpsimd
        def _(eng):
            eng.memset(m["agg"][:, :, :], 0.0).then_inc(cleared, 1)
            eng.wait_ge(wrote, 16)

            def emit(i, a):
                eng.wait_ge(idx_ready[a], i + 1)
                for j in range(BU):
                    s = a * BU + j
                    wait(eng, summed[s], i)
                    eng.sem_inc(begun, 1)
                    for k in range(UT):
                        eng.indirect_dma_start(
                            out=g[s][:, k, :], out_offset=None, in_=m["gtab"][n],
                            in_offset=bass.IndirectOffsetOnAxis(ap=idx[a][:, j * UT + k:j * UT + k + 1], axis=0))\
                           .then_inc(got[s], 16)

            bodies(eng, emit)

        @block.vector
        def _(eng):
            eng.wait_ge(cleared, 1)
            eng.wait_ge(rd_in, 16)

            def places(i, a, j):
                s, q = a * BU + j, j % 2
                o, c = before(i, s, 2, NS)
                wait(eng, summed[o], c)
                for k in range(UT):
                    t = ((2 * i + a) * BU + j) * UT + k
                    eng.tensor_scalar(one[q][:, k, :], m["io128"][:, :],
                                      rd[:, span(t, 1), 1],
                                      None, ALU.is_equal).then_inc(one_ready[s], 1)

            def add(i, a, j):
                s = a * BU + j
                u = (2 * i + a) * BU + j
                b = eng.value_load(m["blkS"][0:1, 1, span(u, 1)], min_val=0, max_val=z.HB - 1)
                eng.wait_ge(summed[s], i + 1)
                o, c = before(i, s, 1, NS)
                wait(eng, added[o], c)
                t = m["agg"][:, bass.ds(b, 1), :].rearrange("p o c -> p (o c)")
                eng.tensor_tensor(t, t, psg[j][:, 0:D], ALU.add).then_inc(added[s], 1)

            def emit(i, a):
                for j in range(BU):
                    places(i, a, j)
                    add(i, a, j)

            bodies(eng, emit)

        @block.tensor
        def _(eng):
            def emit(i, a):
                for j in range(BU):
                    s, q = a * BU + j, j % 2
                    o, c = before(i, s, BU, NS)
                    eng.wait_ge(one_ready[s], (i + 1) * UT)
                    eng.wait_ge(got[s], (i + 1) * 16 * UT)
                    wait(eng, added[o], c)
                    for k in range(UT):
                        mm = eng.matmul(psg[j][:, 0:D], one[q][:, k, :], g[s][:, k, :], start=(k == 0),
                                        stop=(k == UT - 1))
                    mm.then_inc(summed[s], 1)

            bodies(eng, emit)


def close_stage(nc, z, m, sb, ps, sem, n, b, out):
    NB = z.NB
    with ExitStack() as ctx:
        bb = sb(ctx, f"cb{n}", [P, D], fp32)
        v, b_in = sem(ctx, f"v_close{n}"), sem(ctx, f"cb_in{n}")
        norm = Norm(z, ctx, sb, sem, "ln1") if n else None
        normed = sem(ctx, f"normed{n}")
        out_done = sem(ctx, f"out_done{n}")
        block = ctx.enter_context(nc.Block())
        hn, x = m["hn"][:, :, :], m["xn"][:, :, :]

        @block.sync
        def _(eng):
            eng.dma_start(bb[:, :], b.rearrange("(o d) -> o d", o=1).to_broadcast([P, D])).then_inc(b_in, 16)
            if n:
                eng.wait_ge(normed, 1)
                whole = z.N // P
                eng.dma_start(out[0:whole * P, :].rearrange("(b p) d -> p b d", p=P), m["hn"][:, 0:whole, :])\
                   .then_inc(out_done, 16)
                if z.N % P:
                    eng.dma_start(out[whole * P:z.N, :], m["hn"][0:z.N % P, whole, :]).then_inc(out_done, 16)
                eng.wait_ge(out_done, 32 if z.N % P else 16)

        @block.scalar
        def _(eng):
            if n:
                norm.scalar(eng)

        @block.vector
        def _(eng):
            c = Count()

            def done(ins):
                ins.then_inc(v, c.up() and 1)
                eng.wait_ge(v, c.n)

            eng.wait_ge(b_in, 16)
            done(eng.tensor_tensor(hn, m["agg"][:, 0:NB, :], m["gs"][:, :, :], ALU.add))
            done(eng.tensor_tensor(hn, hn, m["dinv"][:, :, None].to_broadcast([P, NB, D]), ALU.mult))
            done(eng.tensor_tensor(hn, hn, bb[:, None, :].to_broadcast([P, NB, D]), ALU.add))
            if n:
                done(eng.scalar_tensor_tensor(x, hn, 0.0, x, ALU.max, ALU.add))
                norm.vector(eng, x, hn, v, c)
                eng.sem_inc(normed, 1)


_INS = ['x', 'src', 'dst', 'edge_attr_64', 'L0_gnn_W', 'L0_gnn_att', 'L0_gnn_bias', 'L0_gnn_bn_gamma',
        'L0_gnn_bn_beta', 'L1_gnn_W1', 'L1_gnn_b1', 'L1_gnn_W2', 'L1_gnn_b2']


def kernel(**inputs):
    import numpy as _np
    import concourse.bacc as _bacc
    from concourse import mybir as _mybir
    from concourse.bass_utils import run_bass_kernel_spmd as _run

    nc = _bacc.Bacc("TRN2", target_bir_lowering=False, num_devices=1)
    arrays, args = {}, []
    for name in _INS:
        a = _np.ascontiguousarray(inputs[name])
        arrays[f"in_{name}_dram"] = a
        args.append(nc.dram_tensor(f"in_{name}_dram", a.shape, _mybir.dt.from_np(a.dtype), kind="ExternalInput").ap())
    shape = inputs['x'].shape
    args.append(nc.dram_tensor("out_0_dram", shape, _mybir.dt.float32, kind="ExternalOutput").ap())
    gnn_kernel(nc, *args)
    r = _run(nc, [arrays], core_ids=[0])
    return r.results[0]["out_0_dram"]
```
